# Optimizing a Trainium2 kernel written in Bass

```python
import numpy as np
import jax
import jax.numpy as jnp

def _softmax(x, axis=-1):
    return jax.nn.softmax(x, axis=axis)

def _gelu(x):
    return jax.nn.gelu(x, approximate=True)

def _silu(x):
    return jax.nn.silu(x)

def _sigmoid(x):
    return jax.nn.sigmoid(x)

def _layernorm(x, axis=-1, eps=1e-05):
    m = jnp.mean(x, axis=axis, keepdims=True)
    v = jnp.var(x, axis=axis, keepdims=True)
    return (x - m) / jnp.sqrt(v + eps)

def _scatter_add(tgt, idx, src, axis=0):
    return tgt.at[idx].add(src)

def _segment_sum(src, seg, n):
    return jax.ops.segment_sum(src, seg, n)
kernel_name = 'mk_flamingo_gated_d1_seqx_r2_539c44'

def setup_inputs(seed: int=0):
    np.random.seed(seed)
    _w = jnp.asarray

    def _rec_inputs():
        import jax
        import jax.numpy as jnp
        _rk = jax.random.key(seed)
        x = 7.22e-05 + 1 * jax.random.normal(jax.random.fold_in(_rk, 1), (16, 256, 2048), jnp.float32)
        _lenS = 256 - jax.random.randint(jax.random.fold_in(_rk, 7), (16,), 0, max(1, 256 // 4) + 1, jnp.int32)
        _lenS2 = 256 - jax.random.randint(jax.random.fold_in(_rk, 8), (16,), 0, max(1, 256 // 4) + 1, jnp.int32)
        _ctx_4096P = jax.random.normal(jax.random.fold_in(_rk, 11), (16, 16, 2048), jnp.float32)
        _ctx_4096c = jax.random.dirichlet(jax.random.fold_in(_rk, 511), 0.3 * jnp.ones((16,), jnp.float32), (16, 256))
        _ctx_4096t = jnp.einsum('bsk,bkd->bsd', _ctx_4096c, _ctx_4096P)
        _ctx_4096t = _ctx_4096t * jax.lax.rsqrt(jnp.mean(jnp.square(_ctx_4096t)) + 1e-12) * 0.953939
        ctx_4096 = 4.13588e-05 + 0.999923 * (_ctx_4096t + 0.3 * jax.random.normal(jax.random.fold_in(_rk, 611), (16, 256, 2048), jnp.float32))
        _g = jax.random.normal(jax.random.fold_in(_rk, 9001), (2, 1), jnp.float32)
        _g = jnp.sign(_g) * jnp.maximum(jnp.abs(_g), 1.0) + (_g == 0) * 1.0
        g_xattn = _g[0]
        g_ffn = _g[1]
        return (x, ctx_4096, g_xattn, g_ffn)
    x, ctx_4096, g_xattn, g_ffn = _rec_inputs()

    def _L0_xattn_setup():
        import jax, jax.numpy as jnp
        import numpy as np
        HEADS = 8
        WINDOW = 16

        def _pointwise(W, b, t):
            return jnp.einsum('oc,bct->bot', W, t) + b[None, :, None]
        key = jax.random.key(seed)
        ks = jax.random.split(key, 10)
        B, C, T = (4, 256, 2048)
        s = 0.02
        return {'x': jax.random.normal(ks[0], (B, C, T), jnp.float32), 'cond': jax.random.normal(ks[1], (B, C, T), jnp.float32), 'Wq': jax.random.normal(ks[2], (C, C), jnp.float32) * s, 'bq': jnp.zeros((C,), jnp.float32), 'Wk': jax.random.normal(ks[3], (C, C), jnp.float32) * s, 'bk': jnp.zeros((C,), jnp.float32), 'Wv': jax.random.normal(ks[4], (C, C), jnp.float32) * s, 'bv': jnp.zeros((C,), jnp.float32), 'Wo': jax.random.normal(ks[5], (C, C), jnp.float32) * s, 'bo': jnp.zeros((C,), jnp.float32)}
    _L0_xattn_all = _L0_xattn_setup()
    _L0_xattn_in = {k: v for k, v in _L0_xattn_all.items() if k in ('Wq', 'bq', 'Wk', 'bk', 'Wv', 'bv', 'Wo', 'bo')}
    del _L0_xattn_all

    def _L0_ffn_setup():
        import jax, jax.numpy as jnp
        import numpy as np
        K_TOP = 8
        key = jax.random.key(seed)
        k1, k2, k3 = jax.random.split(key, 3)
        B, S, H, E = (4, 2048, 2048, 64)
        hidden_states = jax.random.normal(k1, (B, S, H), dtype=jnp.float32)
        router_weight = jax.random.normal(k2, (E, H), dtype=jnp.float32)
        router_bias = jnp.zeros((E,), dtype=jnp.float32)
        expert_bias = jax.random.normal(k3, (E, H), dtype=jnp.float32) * 0.1
        return {'hidden_states': hidden_states, 'router_weight': router_weight, 'router_bias': router_bias, 'expert_bias': expert_bias}
    _L0_ffn_all = _L0_ffn_setup()
    _L0_ffn_in = {k: v for k, v in _L0_ffn_all.items() if k in ('router_weight', 'router_bias', 'expert_bias')}
    del _L0_ffn_all
    return {'x': x, 'ctx_4096': ctx_4096, 'g_xattn': g_xattn, 'g_ffn': g_ffn, 'L0_xattn_Wq': _L0_xattn_in['Wq'], 'L0_xattn_bq': _L0_xattn_in['bq'], 'L0_xattn_Wk': _L0_xattn_in['Wk'], 'L0_xattn_bk': _L0_xattn_in['bk'], 'L0_xattn_Wv': _L0_xattn_in['Wv'], 'L0_xattn_bv': _L0_xattn_in['bv'], 'L0_xattn_Wo': _L0_xattn_in['Wo'], 'L0_xattn_bo': _L0_xattn_in['bo'], 'L0_ffn_router_weight': _L0_ffn_in['router_weight'], 'L0_ffn_router_bias': _L0_ffn_in['router_bias'], 'L0_ffn_expert_bias': _L0_ffn_in['expert_bias']}

def reference(x, ctx_4096, g_xattn, g_ffn, L0_xattn_Wq, L0_xattn_bq, L0_xattn_Wk, L0_xattn_bk, L0_xattn_Wv, L0_xattn_bv, L0_xattn_Wo, L0_xattn_bo, L0_ffn_router_weight, L0_ffn_router_bias, L0_ffn_expert_bias):
    import jax
    import jax.numpy as jnp

    def _L0_xattn_ref(x, cond, Wq, bq, Wk, bk, Wv, bv, Wo, bo):
        import jax, jax.numpy as jnp
        import numpy as np
        HEADS = 8
        WINDOW = 16

        def _pointwise(W, b, t):
            return jnp.einsum('oc,bct->bot', W, t) + b[None, :, None]
        B, C, T = x.shape
        H, W = (HEADS, WINDOW)
        hd = C // H
        scale = hd ** (-0.5)
        pad_left = W // 2
        pad_right = W - pad_left - 1
        q = _pointwise(Wq, bq, x)
        k = _pointwise(Wk, bk, cond)
        v = _pointwise(Wv, bv, cond)
        k = jnp.pad(k, ((0, 0), (0, 0), (pad_left, pad_right)))
        v = jnp.pad(v, ((0, 0), (0, 0), (pad_left, pad_right)))
        idx = jnp.arange(T)[:, None] + jnp.arange(W)[None, :]
        k_win = k[:, :, idx].reshape(B, H, hd, T, W)
        v_win = v[:, :, idx].reshape(B, H, hd, T, W)
        qh = q.reshape(B, H, hd, T)
        dots = jnp.einsum('bhdt,bhdtw->bhtw', qh, k_win) * scale
        attn = jax.nn.softmax(dots, axis=-1)
        out = jnp.einsum('bhtw,bhdtw->bhdt', attn, v_win)
        out = out.reshape(B, C, T)
        return _pointwise(Wo, bo, out)

    def _L0_ffn_ref(hidden_states, router_weight, router_bias, expert_bias):
        import jax, jax.numpy as jnp
        import numpy as np
        K_TOP = 8
        B, S, H = hidden_states.shape
        E = router_weight.shape[0]
        T = B * S
        flat = hidden_states.reshape(T, H)
        logits = jnp.einsum('th,eh->te', flat, router_weight) + router_bias
        scores = jax.nn.softmax(logits, axis=-1)
        topk_w, topk_idx = jax.lax.top_k(scores, K_TOP)
        w_sum = topk_w.sum(axis=-1, keepdims=True)
        w_dense = jnp.zeros((T, E), dtype=scores.dtype).at[jnp.arange(T)[:, None], topk_idx].add(topk_w)
        bias_mix = jnp.einsum('te,eh->th', w_dense, expert_bias)
        out = flat * w_sum + bias_mix
        return out.reshape(B, S, H)
    x = x + jnp.tanh(g_xattn[0]) * _L0_xattn_ref(_layernorm(x, axis=-1), ctx_4096, L0_xattn_Wq, L0_xattn_bq, L0_xattn_Wk, L0_xattn_bk, L0_xattn_Wv, L0_xattn_bv, L0_xattn_Wo, L0_xattn_bo)
    x = x + jnp.tanh(g_ffn[0]) * _L0_ffn_ref(_layernorm(x, axis=-1), L0_ffn_router_weight, L0_ffn_router_bias, L0_ffn_expert_bias)
    return x

_drawn_inputs = setup_inputs


def setup_inputs(seed=0):
    import zlib

    import numpy as np

    out = dict(_drawn_inputs(seed))
    spreads = {'L0_xattn_bq': (0.0, 0.8),
     'L0_xattn_bk': (0.0, 0.8),
     'L0_xattn_bv': (0.0, 0.1),
     'L0_xattn_bo': (0.0, 0.1),
     'L0_ffn_router_bias': (0.0, 0.763)}
    factors = {'L0_xattn_Wq': 4.0, 'L0_xattn_Wk': 4.158}
    for name, (base, spread) in spreads.items():
        noise = np.random.default_rng([zlib.crc32(name.encode()), seed]).standard_normal(out[name].shape)
        drawn = base * np.exp(spread * noise) if base else spread * noise
        out[name] = jnp.asarray(drawn.astype(out[name].dtype))
    for name, factor in factors.items():
        out[name] = (out[name] * factor).astype(out[name].dtype)
    return out
```

```python
from contextlib import ExitStack

import concourse.bass as bass
from concourse import mybir

F32 = mybir.dt.float32
F32R = mybir.dt.float32r
BF16 = mybir.dt.bfloat16
I32 = mybir.dt.int32
ALU = mybir.AluOpType
ACT = mybir.ActivationFunctionType
AX = mybir.AxisListType.X

P = 128
SUB = 32
HPG = 4
WINDOW = 16
LEFT = WINDOW // 2
KEYS = 48
CHUNK = 512
NB = CHUNK // SUB
HALF = NB // 2
UNITS = 4
EPS = 1e-5
NEG = -1e30
RSQRT_SEED = 0x5F3759DF
SCORE_SLOTS = 4


def gated_window_attention_and_router(nc, x, ctx, g_xattn, g_ffn, wqT, bq, wkT, bk, wvT, bv, woT, bo,
                                      wrT, rbias, experts, out):
    B, C, T = x.shape
    G = C // P
    NCH = T // CHUNK
    N = B * NCH
    E = wrT.shape[1]
    TB = CHUNK // P
    HD = C // 8
    SCALE = float(HD) ** -0.5
    assert HD == SUB and G == 2 and NCH == 4 and HPG * HD == P and B % 2 == 0

    with ExitStack() as stack:
        def sb(name, shape, dt=F32):
            return stack.enter_context(nc.sbuf_tensor(name, shape, dt))

        def bank(name):
            return stack.enter_context(nc.psum_tensor(name, [P, 512], F32))

        def sem(name):
            return stack.enter_context(nc.semaphore(name))

        x_in = sb("x_in", [P, G, T])
        x_hi = sb("x_hi", [P, G, CHUNK], F32R)
        x_lo = sb("x_lo", [P, G, CHUNK], F32R)
        c_in = sb("c_in", [P, G, CHUNK])
        c_hi = sb("c_hi", [P, G, CHUNK], F32R)
        c_lo = sb("c_lo", [P, G, CHUNK], F32R)
        x_res = sb("x_res", [P, G, CHUNK])
        wq_raw = sb("wq_raw", [P, G, C])
        w_hi = {k: sb(f"w{k}_hi", [P, G, C], F32R) for k in "qkvo"}
        w_lo = {k: sb(f"w{k}_lo", [P, G, C], F32R) for k in "qkvo"}
        bias = {k: sb(f"b{k}_col", [P, G]) for k in "qkvo"}
        keys = sb("keys", [P, G, LEFT + T + LEFT])
        values = sb("values", [P, G, LEFT + T + SUB - LEFT])
        q_diag = sb("q_diag", [P, G, NB, P])
        v_diag = sb("v_diag", [P, G, NB + 1, P])
        score = sb("score", [P, SCORE_SLOTS, HALF, KEYS])
        prob = sb("prob", [P, 2, HALF, 2 * SUB])
        prob_t = sb("prob_t", [P, G, NB * 2 * SUB])
        att_hi = sb("att_hi", [P, G, CHUNK], F32R)
        att_lo = sb("att_lo", [P, G, CHUNK], F32R)
        x1 = [sb(f"x1_{i}", [P, G, T]) for i in range(2)]
        x1_t = sb("x1_t", [P, G, TB, P])
        wr = sb("wr", [P, T // P, E])
        ex = sb("ex", [E + 1, T])
        ident = sb("ident", [P, P])
        ident_b = sb("ident_b", [P, P], BF16)
        ones = sb("ones", [P, P])
        mask = sb("mask", [P, HALF, KEYS], BF16)
        wr_sum = sb("wr_sum", [P, E])
        rb = sb("rb", [P, E])
        gates = sb("gates", [P, 2])
        gate_a = sb("gate_a", [P, 1])
        gate_f = sb("gate_f", [P, 1])
        st_in = sb("st_in", [P, G, NCH, 6])
        st_x1 = sb("st_x1", [P, G, NCH, 6])
        mv_in = sb("mv_in", [P, G, 2])
        mv_x1 = sb("mv_x1", [P, G, 2])
        half_var = sb("half_var", [P, G])
        rs_in = sb("rs_in", [P, G])
        rs_x1 = sb("rs_x1", [P, G])
        nt = sb("nt", [P, G])
        pad = sb("pad", [P, 6])
        neg_mean_in = sb("neg_mean_in", [P, G])
        neg_mean_x1 = sb("neg_mean_x1", [P, G])
        neg_max = sb("neg_max", [P, UNITS, HALF])
        p_sum = sb("p_sum", [P, UNITS, HALF])
        p_inv = sb("p_inv", [P, UNITS, HALF])
        lg = sb("lg", [P, G, 2, E])
        lg_t = sb("lg_t", [P, G, E])
        top = sb("top", [P, G, 8])
        neg_top = sb("neg_top", [P, G])
        le = sb("le", [P, G, 2, E])
        z_all = sb("z_all", [P, G, 2])
        z_inv = sb("z_inv", [P, G])
        w_sum = sb("w_sum", [P, G])
        row_a = sb("row_a", [P, G])
        wd = sb("wd", [P, G, E + 1])
        wd_t = sb("wd_t", [E + 1, G, P])

        ps_s = [bank(f"ps_s{i}") for i in range(2)]
        ps_a = [bank(f"ps_a{i}") for i in range(G)]
        ps_j = [bank(f"ps_j{i}") for i in range(2)]
        ps_t = bank("ps_t")
        ps_r = bank("ps_r")

        ctx_in = sem("ctx_in")
        x_ld = [sem(f"x_ld{i}") for i in range(NCH)]
        res_in = sem("res_in")
        out_st = [sem(f"out_st{i}") for i in range(G)]
        w_ld = sem("w_ld")
        consts = sem("consts")
        zeros = sem("zeros")
        w_high = sem("w_high")
        w_low = sem("w_low")
        gate_rdy = sem("gate_rdy")
        sum_mm = sem("sum_mm")
        sum_rdy = sem("sum_rdy")
        av_mm = sem("av_mm")
        s_mm = sem("s_mm")
        o_mm = sem("o_mm")
        q_mm = sem("q_mm")
        v_mm = sem("v_mm")
        k_mm = sem("k_mm")
        t_mm = sem("t_mm")
        r_mm = sem("r_mm")
        wt_mm = sem("wt_mm")
        mix_mm = sem("mix_mm")
        xh_rdy = sem("xh_rdy")
        ch_rdy = sem("ch_rdy")
        ah_rdy = sem("ah_rdy")
        e_rdy = sem("e_rdy")
        q_rdy = sem("q_rdy")
        v_rdy = sem("v_rdy")
        k_rdy = sem("k_rdy")
        xt_rdy = sem("xt_rdy")
        le_rdy = sem("le_rdy")
        wt_rdy = sem("wt_rdy")
        wqh_rdy = sem("wqh_rdy")
        xl_rdy = sem("xl_rdy")
        al_rdy = sem("al_rdy")
        vd_rdy = sem("vd_rdy")
        mx_rdy = sem("mx_rdy")
        sh_rdy = sem("sh_rdy")
        su_rdy = sem("su_rdy")
        iv_rdy = sem("iv_rdy")
        pt_rdy = sem("pt_rdy")
        x1_rdy = sem("x1_rdy")
        st1_rdy = sem("st1_rdy")
        st2_rdy = sem("st2_rdy")
        ln1_rdy = sem("ln1_rdy")
        ln2_rdy = sem("ln2_rdy")
        small = sem("small")
        aggr1 = sem("aggr1")
        aggr2 = sem("aggr2")
        wsum_rdy = sem("wsum_rdy")
        lg_rdy = sem("lg_rdy")
        wd_rdy = sem("wd_rdy")
        wql_rdy = sem("wql_rdy")
        fin_rdy = sem("fin_rdy")
        cl_rdy = sem("cl_rdy")
        pm_rdy = sem("pm_rdy")

        def done(per, b, c, off, i):
            return b * (per * NCH) + (per * (c + off) + i + 1)

        def live(b, c, off):
            return not isinstance(b, int) or 0 <= NCH * b + c + off < N

        def final(b, g, j):
            return (b + 1) * (NCH * G) + NCH * g + j + 1

        def seq(b):
            return not isinstance(b, int) or 0 <= b < B

        def need(eng, s, value):
            if not isinstance(value, int) or value > 0:
                eng.wait_ge(s, value)

        def walk(eng, step):
            for c in (2, 3):
                step(-1, c, 1)
            for c in range(NCH):
                step(0, c, 0)
            with eng.Fori(1, B - 3, 2) as b:
                for c in range(NCH):
                    step(b, c, 1)
                for c in range(NCH):
                    step(b + 1, c, 0)
            for b in range(B - 3, B + 1):
                for c in range(NCH):
                    step(b, c, b % 2)

        def place(c, off):
            return (c + off) % NCH, (c + off) // NCH

        def cols(ch):
            return slice(ch * CHUNK, (ch + 1) * CHUNK)

        block = stack.enter_context(nc.Block())

        @block.sync
        def _(sp):
            sp.dma_start(x_in[:, :, cols(0)], x[0, :, cols(0)].rearrange("(g p) t -> p g t", g=G)).then_inc(x_ld[0], 16)
            sp.dma_start(c_in[:], ctx[0, :, cols(0)].rearrange("(g p) t -> p g t", g=G)).then_inc(ctx_in, 16)
            for ch in range(1, NCH):
                sp.dma_start(x_in[:, :, cols(ch)],
                             x[0, :, cols(ch)].rearrange("(g p) t -> p g t", g=G)).then_inc(x_ld[ch], 16)
            sp.dma_start(wq_raw[:], wqT.rearrange("(g p) o -> p g o", g=G)).then_inc(w_ld, 16)
            for i, w in enumerate((wkT, wvT, woT)):
                sp.dma_start(x1[1][:, :, i * C:(i + 1) * C], w.rearrange("(g p) o -> p g o", g=G)).then_inc(w_ld, 16)
            for k, v in zip("qkvo", (bq, bk, bv, bo)):
                sp.dma_start(bias[k][:], v).then_inc(w_ld, 16)
            sp.dma_start(gates[:, 0:1], g_xattn.partition_broadcast(P)).then_inc(w_ld, 16)
            sp.dma_start(gates[:, 1:2], g_ffn.partition_broadcast(P)).then_inc(w_ld, 16)
            sp.dma_start(rb[:], rbias.partition_broadcast(P)).then_inc(w_ld, 16)
            sp.dma_start(wr[:], wrT.rearrange("(n p) e -> p n e", p=P)).then_inc(w_ld, 16)
            sp.dma_start(ex[0:E, :], experts).then_inc(w_ld, 16)

            def address(ap):
                if not isinstance(ap.offset, int):
                    sp.to_reg(ap.offset * 4)
                return ap

            def step(b, c, par):
                if live(b, c, 3) and live(b, c, 2):
                    ch, db = place(c, 3)
                    rows_in = address(ctx[b + db, :, cols(ch)].rearrange("(g p) t -> p g t", g=G))
                    need(sp, cl_rdy, done(1, b, c, 2, 0))
                    sp.dma_start(c_in[:], rows_in).then_inc(ctx_in, 16)
                if live(b, c, 5) and live(b, c, 1):
                    ch, db = place(c, 5)
                    rows_in = address(x[b + db, :, cols(ch)].rearrange("(g p) t -> p g t", g=G))
                    need(sp, xl_rdy, done(2, b, c, 1, 1))
                    sp.dma_start(x_in[:, :, cols(ch)], rows_in).then_inc(x_ld[ch], 16)
                if live(b, c, 0):
                    rows_in = address(x[b, :, cols(c)].rearrange("(g p) t -> p g t", g=G))
                    need(sp, x1_rdy, done(2, b, c, -1, 1))
                    sp.dma_start(x_res[:], rows_in).then_inc(res_in, 16)
                if c >= 2 and seq(b - 1):
                    g = c - 2
                    rows_out = address(out[b - 1, g * P:(g + 1) * P, :])
                    need(sp, fin_rdy, final(b - 1, g, NCH - 1))
                    sp.dma_start(rows_out, x1[1 - par][:, g, :]).then_inc(out_st[g], 16)

            walk(sp, step)
            for g in range(G):
                sp.wait_ge(out_st[g], 16 * (B + 1))
            sp.wait_ge(w_ld, 16 * 13)

        @block.gpsimd
        def _(pool):
            pool.memset(keys[:], 0.0).then_inc(zeros, 1)
            pool.memset(values[:], 0.0).then_inc(zeros, 1)
            pool.memset(ident[:], 0.0).then_inc(consts, 1)
            pool.memset(ident_b[:], 0.0).then_inc(consts, 1)
            pool.memset(mask[:], 0.0).then_inc(consts, 1)
            pool.wait_ge(consts, 3)
            pool.affine_select(out=ident[:], in_=ident[:], compare_op=ALU.not_equal, fill=1.0, base=0,
                               pattern=[[-1, P]], channel_multiplier=1).then_inc(consts, 1)
            pool.affine_select(out=ident_b[:], in_=ident_b[:], compare_op=ALU.not_equal, fill=1.0, base=0,
                               pattern=[[-1, P]], channel_multiplier=1).then_inc(consts, 1)
            pool.wait_ge(consts, 5)
            for h in range(HPG):
                m = mask[SUB * h:SUB * (h + 1)]
                pool.affine_select(out=m, in_=m, compare_op=ALU.is_ge, fill=NEG, base=0,
                                   pattern=[[0, HALF], [1, KEYS]], channel_multiplier=-1).then_inc(consts, 1)
                pool.wait_ge(consts, 6 + 2 * h)
                pool.affine_select(out=m, in_=m, compare_op=ALU.is_ge, fill=NEG, base=WINDOW - 1,
                                   pattern=[[0, HALF], [-1, KEYS]], channel_multiplier=1).then_inc(consts, 1)
                pool.wait_ge(consts, 7 + 2 * h)
            pool.memset(ones[:], 1.0).then_inc(consts, 1)
            pool.memset(q_diag[:], 0.0).then_inc(zeros, 1)
            pool.memset(v_diag[:], 0.0).then_inc(zeros, 1)
            pool.memset(prob[:], 0.0).then_inc(zeros, 1)
            pool.wait_ge(zeros, 5)
            pool.memset(ex[E:E + 1, :], 1.0).then_inc(consts, 1)
            pool.wait_ge(consts, 15)

            def step(b, c, par):
                if live(b, c, 2):
                    need(pool, ch_rdy, done(1, b, c, 2, 0))
                    pool.tensor_tensor(c_lo[:], c_in[:], c_hi[:], ALU.subtract).then_inc(cl_rdy, 1)
                if live(b, c, 0):
                    for u in range(UNITS):
                        need(pool, iv_rdy, done(UNITS, b, c, 0, u))
                        need(pool, pt_rdy, done(UNITS, b, c, 0, u - 2))
                        pool.tensor_tensor(prob[:, u % 2, :, 0:KEYS], score[:, u],
                                           p_inv[:, u, :].unsqueeze(2).to_broadcast([P, HALF, KEYS]),
                                           ALU.mult).then_inc(pm_rdy, 1)

            walk(pool, step)

        @block.scalar
        def _(act):
            act.wait_ge(w_ld, 16 * 13)
            act.activation(gate_a[:], gates[:, 0:1], ACT.Tanh).then_inc(gate_rdy, 1)
            act.activation(gate_f[:], gates[:, 1:2], ACT.Tanh).then_inc(gate_rdy, 1)
            act.wait_ge(gate_rdy, 3)
            for i, k in enumerate("kvo"):
                act.activation(w_hi[k][:], x1[1][:, :, i * C:(i + 1) * C], ACT.Copy,
                               ).then_inc(w_high, 1)
            act.wait_ge(zeros, 5)

            def step(b, c, par):
                if c == 3 and seq(b + 1):
                    need(act, ln1_rdy, b + 2)
                    need(act, q_mm, done(2, b, c, 0, 1))
                    for g in range(G):
                        act.activation(w_hi["q"][:, g], wq_raw[:, g], ACT.Copy, scale=rs_in[:, g:g + 1]).then_inc(wqh_rdy, 1)
                if live(b, c, 1):
                    ch, db = place(c, 1)
                    for g in range(G):
                        if g == 0:
                            need(act, x_ld[ch], (b + db + 1) * 16)
                            need(act, ln1_rdy, b + db + 1)
                            need(act, q_mm, done(2, b, c, 0, 1))
                        act.activation(x_hi[:, g], x_in[:, g, cols(ch)], ACT.Identity,
                                       bias=neg_mean_in[:, g:g + 1]).then_inc(xh_rdy, 1)
                if live(b, c, 2):
                    need(act, ctx_in, done(1, b, c, 2, 0) * 16)
                    need(act, k_mm, done(2, b, c, 1, 1))
                    need(act, cl_rdy, done(1, b, c, 1, 0))
                    act.activation(c_hi[:], c_in[:], ACT.Copy).then_inc(ch_rdy, 1)
                if live(b, c, -1):
                    for g in range(G):
                        need(act, av_mm, done(2, b, c, -1, g))
                        need(act, o_mm, done(2, b, c, -2, 1))
                        need(act, al_rdy, done(2, b, c, -2, g))
                        act.activation(att_hi[:, g], ps_a[g][:], ACT.Copy).then_inc(ah_rdy, 1)
                if c == 1 and seq(b - 1):
                    need(act, lg_rdy, b * G)
                    for g in range(G):
                        for j in range(2):
                            act.activation(le[:, g, j], lg[:, g, j], ACT.Exp, bias=neg_top[:, g:g + 1],
                                           accum_out=z_all[:, g, j:j + 1]).then_inc(le_rdy, 1)
                if live(b, c, 0):
                    for u in range(UNITS):
                        if u == 2 and c == 2 and seq(b - 1):
                            need(act, wt_mm, b)
                            act.activation(wd_t[:], ps_t[0:E + 1, 0:G * P].rearrange("e (g p) -> e g p", g=G),
                                           ACT.Copy).then_inc(wt_rdy, 1)
                        need(act, sh_rdy, done(UNITS, b, c, 0, u))
                        act.activation(score[:, u], score[:, u], ACT.Exp, scale=SCALE).then_inc(e_rdy, 1)
                elif c == 2 and seq(b - 1):
                    need(act, wt_mm, b)
                    act.activation(wd_t[:], ps_t[0:E + 1, 0:G * P].rearrange("e (g p) -> e g p", g=G),
                                   ACT.Copy).then_inc(wt_rdy, 1)

                def copy_rows(g):
                    need(act, t_mm, done(2, b, c, -1, g))
                    need(act, r_mm, done(1, b, c, -2, 0))
                    act.activation(x1_t[:, g], ps_t[:].rearrange("p (k t) -> p k t", k=TB), ACT.Copy).then_inc(xt_rdy, 1)

                if live(b, c, -1):
                    copy_rows(0)
                if live(b, c, 1):
                    for g in range(G):
                        need(act, q_mm, done(2, b, c, 1, g))
                        need(act, s_mm, done(UNITS, b, c, 0, UNITS - 1))
                        for h in range(HPG):
                            r = slice(SUB * h, SUB * (h + 1))
                            act.activation(q_diag[r, g, :, r], ps_j[g][r, :].rearrange("p (n i) -> p n i", i=SUB),
                                           ACT.Identity, bias=bias["q"][r, g:g + 1]).then_inc(q_rdy, 1)
                if live(b, c, 2):
                    ch, _ = place(c, 2)
                    at = slice(LEFT + ch * CHUNK, LEFT + (ch + 1) * CHUNK)
                    for g in range(G):
                        need(act, v_mm, done(2, b, c, 2, g))
                        need(act, vd_rdy, done(8, b, c, -1, 7))
                        act.activation(values[:, g, at], ps_j[g][:], ACT.Identity,
                                       bias=bias["v"][:, g:g + 1]).then_inc(v_rdy, 1)
                if live(b, c, -1):
                    copy_rows(1)
                if live(b, c, 2):
                    for g in range(G):
                        need(act, k_mm, done(2, b, c, 2, g))
                        need(act, s_mm, done(UNITS, b, c, -1, UNITS - 1))
                        act.activation(keys[:, g, at], ps_j[g][:], ACT.Identity,
                                       bias=bias["k"][:, g:g + 1]).then_inc(k_rdy, 1)

            walk(act, step)

        @block.vector
        def _(dve):
            def inverse_root(base, mv, rs, neg_mean, ready):
                k = [0]

                def link(ins):
                    k[0] += 1
                    ins.then_inc(small, 1)
                    dve.wait_ge(small, base + k[0])

                link(dve.tensor_scalar(half_var[:], mv[:, :, 1], EPS, None, ALU.add))
                link(dve.tensor_scalar(rs[:].bitcast(I32), half_var[:].bitcast(I32), -0.5, float(RSQRT_SEED),
                                       ALU.mult, ALU.add))
                link(dve.tensor_scalar(half_var[:], half_var[:], -0.5, None, ALU.mult))
                for _ in range(3):
                    link(dve.tensor_tensor(nt[:], rs[:], rs[:], ALU.mult))
                    link(dve.tensor_tensor(nt[:], nt[:], half_var[:], ALU.mult))
                    link(dve.tensor_scalar(nt[:], nt[:], 1.5, None, ALU.add))
                    link(dve.tensor_tensor(rs[:], rs[:], nt[:], ALU.mult))
                assert k[0] == NEWTON
                dve.tensor_scalar(neg_mean[:], mv[:, :, 0], -1.0, None, ALU.mult).then_inc(ready, 1)

            NEWTON = 15
            ROUTER = 12

            dve.wait_ge(gate_rdy, 2)
            dve.wait_ge(w_ld, 16 * 13)
            wo_staged = x1[1][:, :, 2 * C:3 * C]
            dve.tensor_scalar(wo_staged, wo_staged, gate_a[:], None, ALU.mult).then_inc(gate_rdy, 1)
            dve.tensor_scalar(bias["o"][:], bias["o"][:], gate_a[:], None, ALU.mult).then_inc(sum_rdy, 1)
            for i, k in enumerate("kvo"):
                dve.wait_ge(w_high, i + 1)
                dve.tensor_tensor(w_lo[k][:], x1[1][:, :, i * C:(i + 1) * C], w_hi[k][:], ALU.subtract).then_inc(w_low, 1)
            dve.wait_ge(sum_mm, 1)
            dve.tensor_copy(wr_sum[:], ps_r[:, 0:E]).then_inc(sum_rdy, 1)
            dve.memset(pad[:, 3:4], 0.0).then_inc(fin_rdy, NCH * G)
            for g in range(G):
                dve.memset(pad[:, 4 + g:5 + g], 0.0).then_inc(out_st[g], 16)

            dve.wait_ge(sum_rdy, 2)
            dve.wait_ge(zeros, 5)

            def stats_in(ch):
                for g in range(G):
                    dve.bn_stats(st_in[:, g, ch], x_in[:, g, cols(ch)]).then_inc(st1_rdy, 1)

            def ln1(b, base):
                need(dve, st1_rdy, b * (NCH * G) + NCH * G)
                dve.memset(pad[:, 1:2], 0.0).then_inc(aggr1, 1)
                for g in range(G):
                    dve.bn_aggr(mv_in[:, g], st_in[:, g]).then_inc(aggr1, 1)
                need(dve, aggr1, (b + 1) * (G + 1))
                inverse_root(base, mv_in, rs_in, neg_mean_in, ln1_rdy)

            for ch in range(NCH):
                dve.wait_ge(x_ld[ch], 16)
                stats_in(ch)
            ln1(0, 0)

            def small_base(b, which):
                per = 2 * NEWTON + ROUTER
                start = b * per + (2 * NEWTON - per)
                if isinstance(b, int) and b == 0:
                    return NEWTON
                if isinstance(b, int) and b == B:
                    start -= NEWTON
                return start + (0, NEWTON, NEWTON + ROUTER)[which]

            def step(b, c, par):
                if c == 3 and seq(b + 1):
                    need(dve, wqh_rdy, (b + 2) * G)
                    for g in range(G):
                        dve.scalar_tensor_tensor(w_lo["q"][:, g], wq_raw[:, g], rs_in[:, g:g + 1], w_hi["q"][:, g],
                                                 ALU.mult, ALU.subtract).then_inc(wql_rdy, 1)
                if live(b, c, 1):
                    ch, _ = place(c, 1)
                    for g in range(G):
                        need(dve, xh_rdy, done(2, b, c, 1, g))
                        dve.scalar_tensor_tensor(x_lo[:, g], x_in[:, g, cols(ch)], mv_in[:, g, 0:1], x_hi[:, g],
                                                 ALU.subtract, ALU.subtract).then_inc(xl_rdy, 1)
                if c == 1 and seq(b - 1):
                    router_logits(b)
                for g in range(G):
                    if live(b, c, -1):
                        need(dve, ah_rdy, done(2, b, c, -1, g))
                        dve.tensor_tensor(att_lo[:, g], ps_a[g][:], att_hi[:, g], ALU.subtract).then_inc(al_rdy, 1)
                    if live(b, c, 0):
                        if g == 0:
                            need(dve, v_rdy, done(2, b, c, 1 if live(b, c, 1) else 0, 1))
                        need(dve, av_mm, done(2, b, c, -1, g))
                        for h in range(HPG):
                            r = slice(SUB * h, SUB * (h + 1))
                            dve.transpose(v_diag[r, g, :, r],
                                          values[r, g, c * CHUNK:(c + 1) * CHUNK + SUB].rearrange("p (n i) -> p n i", i=SUB)
                                          ).then_inc(vd_rdy, 1)

                def shift(u):
                    s = ps_s[u % 2][:, 0:HALF * KEYS].rearrange("p (n k) -> p n k", k=KEYS)
                    need(dve, s_mm, done(UNITS, b, c, 0, u))
                    dve.tensor_reduce(neg_max[:, u], s, AX, ALU.max, negate=True).then_inc(mx_rdy, 1)
                    need(dve, mx_rdy, done(UNITS, b, c, 0, u))
                    need(dve, pm_rdy, done(UNITS, b, c, 0, u - SCORE_SLOTS))
                    dve.tensor_tensor(score[:, u], s, neg_max[:, u, :].unsqueeze(2).to_broadcast([P, HALF, KEYS]),
                                      ALU.add).then_inc(sh_rdy, 1)

                def invert(u):
                    need(dve, e_rdy, done(UNITS, b, c, 0, u))
                    dve.tensor_reduce(p_sum[:, u], score[:, u], AX, ALU.add).then_inc(su_rdy, 1)
                    need(dve, su_rdy, done(UNITS, b, c, 0, u))
                    dve.reciprocal(p_inv[:, u], p_sum[:, u]).then_inc(iv_rdy, 1)

                def turn(u):
                    need(dve, pm_rdy, done(UNITS, b, c, 0, u))
                    need(dve, av_mm, done(2, b, c, -1, u // 2))
                    dve.transpose(prob_t[:, u // 2, (u % 2) * CHUNK:(u % 2 + 1) * CHUNK],
                                  prob[:, u % 2].rearrange("p n k -> p (n k)")).then_inc(pt_rdy, 1)

                def residual(g):
                    ch, db = place(c, -1)
                    buf = x1[(par if db == 0 else 1 - par)]
                    need(dve, o_mm, done(2, b, c, -1, g))
                    need(dve, res_in, done(1, b, c, -1, 0) * 16)
                    if ch == 0:
                        need(dve, out_st[g], b * 16)
                    dve.scalar_tensor_tensor(buf[:, g, cols(ch)], ps_j[g][:], bias["o"][:, g:g + 1], x_res[:, g],
                                             ALU.add, ALU.add).then_inc(x1_rdy, 1)

                def stats_x1(g):
                    ch, db = place(c, -1)
                    buf = x1[(par if db == 0 else 1 - par)]
                    need(dve, x1_rdy, done(2, b, c, -1, g))
                    dve.bn_stats(st_x1[:, g, ch], buf[:, g, cols(ch)]).then_inc(st2_rdy, 1)

                if live(b, c, 0):
                    shift(0)
                    shift(1)
                if live(b, c, -1):
                    residual(0)
                    residual(1)
                if live(b, c, 0):
                    shift(2)
                    invert(0)
                    shift(3)
                    invert(1)
                if live(b, c, -1):
                    stats_x1(0)
                if live(b, c, 0):
                    turn(0)
                    invert(2)
                    turn(1)
                    invert(3)
                if live(b, c, -1):
                    stats_x1(1)
                if c == 1 and seq(b - 1):
                    router_weights(b)
                if live(b, c, 0):
                    turn(2)
                    turn(3)
                if live(b, c, 5) and live(b, c, 1):
                    ch, db = place(c, 5)
                    need(dve, x_ld[ch], (b + db + 1) * 16)
                    stats_in(ch)
                if c == 2 and seq(b + 1) and not (isinstance(b, int) and b < 0):
                    ln1(b + 1, small_base(b, 2))
                if c == 0 and seq(b - 1):
                    need(dve, st2_rdy, b * (NCH * G))
                    dve.memset(pad[:, 2:3], 0.0).then_inc(aggr2, 1)
                    for g in range(G):
                        dve.bn_aggr(mv_x1[:, g], st_x1[:, g]).then_inc(aggr2, 1)
                    need(dve, aggr2, b * (G + 1))
                    inverse_root(small_base(b, 0), mv_x1, rs_x1, neg_mean_x1, ln2_rdy)
                if c >= 2 and seq(b - 1):
                    g = c - 2
                    buf = x1[1 - par]
                    for j in range(NCH):
                        need(dve, mix_mm, (b - 1) * (NCH * G) + NCH * g + j + 1)
                        dve.scalar_tensor_tensor(buf[:, g, cols(j)], buf[:, g, cols(j)], row_a[:, g:g + 1],
                                                 ps_j[j % 2][:], ALU.mult, ALU.add).then_inc(fin_rdy, 1)

            def router_logits(b):
                base = small_base(b, 1)
                need(dve, r_mm, (b - 1) * NCH + NCH)
                need(dve, ln2_rdy, b)
                for g in range(G):
                    dve.scalar_tensor_tensor(lg_t[:, g], wr_sum[:], neg_mean_x1[:, g:g + 1], ps_r[:, g * E:(g + 1) * E],
                                             ALU.mult, ALU.add).then_inc(small, 1)
                dve.wait_ge(small, base + 2)
                for g in range(G):
                    dve.scalar_tensor_tensor(lg[:, g, 0], lg_t[:, g], rs_x1[:, g:g + 1], rb[:],
                                             ALU.mult, ALU.add).then_inc(small, 1)
                dve.wait_ge(small, base + 4)
                dve.memset(pad[:, 0:1], 0.0).then_inc(small, 1)
                for g in range(G):
                    dve.max(top[:, g], lg[:, g, 0]).then_inc(small, 1)
                dve.wait_ge(small, base + 7)
                dve.tensor_scalar(neg_top[:], top[:, :, 0], -1.0, None, ALU.mult).then_inc(small, 1)
                dve.match_replace(lg[:, 0, 1], top[:, 0], lg[:, 0, 0], NEG).then_inc(lg_rdy, 1)
                dve.match_replace(lg[:, 1, 1], top[:, 1], lg[:, 1, 0], NEG).then_inc(lg_rdy, 1)

            def router_weights(b):
                base = small_base(b, 1)
                need(dve, le_rdy, b * (2 * G))
                need(dve, lg_rdy, b * G)
                dve.reciprocal(z_inv[:], z_all[:, :, 0]).then_inc(small, 1)
                dve.tensor_tensor(lg_t[:], le[:, :, 0], le[:, :, 1], ALU.subtract).then_inc(small, 1)
                dve.wait_ge(small, base + 10)
                dve.tensor_scalar(z_inv[:], z_inv[:], gate_f[:], None, ALU.mult).then_inc(small, 1)
                dve.wait_ge(small, base + 11)
                dve.tensor_tensor(wd[:, :, 0:E], lg_t[:], z_inv[:].unsqueeze(2).to_broadcast([P, G, E]),
                                  ALU.mult).then_inc(small, 1)
                dve.wait_ge(small, base + 12)
                dve.tensor_reduce(w_sum[:], wd[:, :, 0:E], AX, ALU.add).then_inc(wsum_rdy, 1)
                need(dve, wsum_rdy, 3 * b - 2)
                dve.tensor_tensor(w_sum[:], w_sum[:], rs_x1[:], ALU.mult).then_inc(wsum_rdy, 1)
                need(dve, wsum_rdy, 3 * b - 1)
                dve.tensor_scalar(row_a[:], w_sum[:], 1.0, None, ALU.add).then_inc(wsum_rdy, 1)
                dve.tensor_tensor(wd[:, :, E:E + 1].rearrange("p g o -> p (g o)"), w_sum[:], neg_mean_x1[:],
                                  ALU.mult).then_inc(wd_rdy, 1)

            walk(dve, step)

        @block.tensor
        def _(pe):
            pe.wait_ge(w_ld, 16 * 13)
            pe.wait_ge(consts, 15)
            for i in range(T // P):
                ins = pe.matmul(ps_r[:, 0:E], ones[:], wr[:, i], start=(i == 0), stop=(i == T // P - 1))
            ins.then_inc(sum_mm, 1)
            pe.wait_ge(w_low, 3)

            def project(dst, k, g, hi, lo):
                o = slice(g * P, (g + 1) * P)
                terms = [(w_hi[k], hi), (w_lo[k], hi), (w_hi[k], lo)]
                n = 0
                for w, v in terms:
                    for i in range(G):
                        ins = pe.matmul(dst[:], w[:, i, o], v[:, i], start=(n == 0), stop=(n == 2 * G + 1))
                        n += 1
                return ins

            def step(b, c, par):
                if live(b, c, -1):
                    for g in range(G):
                        need(pe, pt_rdy, done(UNITS, b, c, -1, 2 * g + 1))
                        need(pe, vd_rdy, done(8, b, c, -1, 4 * g + 3))
                        need(pe, al_rdy, done(2, b, c, -2, g))
                        for j in range(NB + 1):
                            lo = max(0, (2 * j - 1) * SUB)
                            hi = min(2 * NB * SUB, (2 * j + 1) * SUB)
                            q0 = max(0, (j - 1) * SUB)
                            q1 = min(CHUNK, (j + 1) * SUB)
                            ins = pe.matmul(ps_a[g][:, q0:q1], v_diag[:, g, j], prob_t[:, g, lo:hi],
                                            start=(j == 0), stop=(j == NB), skip_group_check=True)
                        ins.then_inc(av_mm, 1)

                def scores(u):
                    g, half = u // 2, u % 2
                    need(pe, sh_rdy, done(UNITS, b, c, 0, u - 2))
                    s = ps_s[u % 2]
                    pe.matmul(s[:, 0:HALF * KEYS], ident_b[:], mask[:].rearrange("p n k -> p (n k)"),
                              start=True, stop=False)
                    for n in range(HALF):
                        tb = half * HALF + n
                        at = c * CHUNK + tb * SUB
                        ins = pe.matmul(s[:, n * KEYS:(n + 1) * KEYS], q_diag[:, g, tb], keys[:, g, at:at + KEYS],
                                        start=False, stop=(n == HALF - 1))
                    ins.then_inc(s_mm, 1)

                if live(b, c, 0):
                    need(pe, q_rdy, done(8, b, c, 0, 7))
                    need(pe, k_rdy, done(2, b, c, 1 if live(b, c, 1) else 0, 1))
                    scores(0)
                    scores(1)
                if c == 2 and seq(b - 1):
                    need(pe, wd_rdy, b)
                    need(pe, xt_rdy, done(2, b, c, -2, 1) if live(b, c, -2) else 2 * N)
                    for g in range(G):
                        ins = pe.transpose(ps_t[0:E + 1, g * P:(g + 1) * P], wd[:, g], ident[:])
                    ins.then_inc(wt_mm, 1)
                if live(b, c, -1):
                    for g in range(G):
                        if g == 0:
                            need(pe, al_rdy, done(2, b, c, -1, 1))
                        if live(b, c, 1):
                            need(pe, k_rdy, done(2, b, c, 1, g))
                        if c in (0, 3):
                            bb = b - 1 if c == 3 else b - 2
                            if seq(bb):
                                need(pe, fin_rdy, final(bb, 0 if c == 3 else 1, 2 + g))
                        project(ps_j[g], "o", g, att_hi, att_lo).then_inc(o_mm, 1)
                if live(b, c, 0):
                    scores(2)
                    scores(3)

                def rows(g):
                    ch, db = place(c, -1)
                    buf = x1[(par if db == 0 else 1 - par)]
                    need(pe, x1_rdy, done(2, b, c, -1, g))
                    need(pe, xt_rdy, done(2, b, c, -1, g - 1))
                    if c == 2 and seq(b - 1):
                        need(pe, wt_rdy, b)
                    for k in range(TB):
                        t = ch * CHUNK + k * P
                        ins = pe.transpose(ps_t[:, k * P:(k + 1) * P], buf[:, g, t:t + P], ident[:])
                    ins.then_inc(t_mm, 1)

                if live(b, c, -1):
                    rows(0)
                if live(b, c, 1):
                    for g in range(G):
                        need(pe, xl_rdy, done(2, b, c, 1, 1))
                        need(pe, wql_rdy, (b + place(c, 1)[1] + 1) * G)
                        need(pe, x1_rdy, done(2, b, c, -1, g))
                        if not live(b, c, -1):
                            need(pe, k_rdy, done(2, b, c, 1, g))
                        project(ps_j[g], "q", g, x_hi, x_lo).then_inc(q_mm, 1)
                if live(b, c, 2):
                    for g in range(G):
                        need(pe, cl_rdy, done(1, b, c, 2, 0))
                        if live(b, c, 1):
                            need(pe, q_rdy, done(8, b, c, 1, 4 * g + 3))
                        project(ps_j[g], "v", g, c_hi, c_lo).then_inc(v_mm, 1)
                if live(b, c, -1):
                    rows(1)
                if live(b, c, 2):
                    for g in range(G):
                        need(pe, v_rdy, done(2, b, c, 2, g))
                        project(ps_j[g], "k", g, c_hi, c_lo).then_inc(k_mm, 1)
                if c >= 2 and seq(b - 1):
                    g = c - 2
                    need(pe, wt_rdy, b)
                    for j in range(NCH):
                        if j < 2:
                            if live(b, c, 2):
                                need(pe, k_rdy, done(2, b, c, 2, j))
                            elif live(b, c, 1):
                                need(pe, q_rdy, done(8, b, c, 1, 4 * j + 3))
                            elif live(b, c, -1):
                                need(pe, x1_rdy, done(2, b, c, -1, j))
                            else:
                                need(pe, fin_rdy, final(b - 1, g, j - 2))
                        else:
                            need(pe, fin_rdy, final(b - 1, g, j - 2))
                        pe.matmul(ps_j[j % 2][:], wd_t[:, g], ex[:, cols(j)], start=True, stop=True).then_inc(mix_mm, 1)
                if live(b, c, -1):
                    ch, db = place(c, -1)
                    need(pe, xt_rdy, done(2, b, c, -1, 1))
                    if ch == 0:
                        need(pe, lg_rdy, b * G)
                        if isinstance(b, int) and b == 0:
                            need(pe, sum_rdy, 2)
                    for k in range(TB):
                        for g in range(G):
                            ins = pe.matmul(ps_r[:, g * E:(g + 1) * E], x1_t[:, g, k], wr[:, ch * TB + k],
                                            start=(ch == 0 and k == 0 and g == 0),
                                            stop=(ch == NCH - 1 and k == TB - 1), skip_group_check=True)
                    ins.then_inc(r_mm, 1)

            walk(pe, step)


def kernel(**inputs):
    import numpy as np
    import concourse.bacc as bacc
    from concourse import mybir as _mybir
    from concourse.bass_utils import run_bass_kernel_spmd as run

    a = {k: np.asarray(v) for k, v in inputs.items()}
    col = lambda v: np.ascontiguousarray(v.reshape(2, 128).T)
    arrays = {
        "x_dram": a["x"], "ctx_dram": a["ctx_4096"], "g_xattn_dram": a["g_xattn"], "g_ffn_dram": a["g_ffn"],
        "wqT_dram": a["L0_xattn_Wq"].T, "bq_dram": col(a["L0_xattn_bq"]),
        "wkT_dram": a["L0_xattn_Wk"].T, "bk_dram": col(a["L0_xattn_bk"]),
        "wvT_dram": a["L0_xattn_Wv"].T, "bv_dram": col(a["L0_xattn_bv"]),
        "woT_dram": a["L0_xattn_Wo"].T, "bo_dram": col(a["L0_xattn_bo"]),
        "wrT_dram": a["L0_ffn_router_weight"].T, "rbias_dram": a["L0_ffn_router_bias"],
        "experts_dram": a["L0_ffn_expert_bias"],
    }
    arrays = {k: np.ascontiguousarray(v) for k, v in arrays.items()}
    nc = bacc.Bacc("TRN2", target_bir_lowering=False, num_devices=1)
    args = [nc.dram_tensor(k, v.shape, _mybir.dt.from_np(v.dtype), kind="ExternalInput").ap() for k, v in arrays.items()]
    args.append(nc.dram_tensor("out_dram", a["x"].shape, _mybir.dt.float32, kind="ExternalOutput").ap())
    gated_window_attention_and_router(nc, *args)
    r = run(nc, [arrays], core_ids=[0])
    return r.results[0]["out_dram"]
```

```python
from contextlib import ExitStack

import concourse.bass as bass
from concourse import mybir

F32 = mybir.dt.float32
F32R = mybir.dt.float32r
BF16 = mybir.dt.bfloat16
F16 = mybir.dt.float16
I32 = mybir.dt.int32
ALU = mybir.AluOpType
ACT = mybir.ActivationFunctionType
AX = mybir.AxisListType.X

P = 128
SUB = 32
HPG = 4
WINDOW = 16
LEFT = WINDOW // 2
KEYS = 48
CHUNK = 512
NB = CHUNK // SUB
HALF = NB // 2
UNITS = 4
EPS = 1e-5
NEG = -1e30
RSQRT_SEED = 0x5F3759DF
SCORE_SLOTS = 4
TOP = 2.0 ** 14
TINY = 1e-30


def gated_window_attention_and_router(nc, x, ctx, g_xattn, g_ffn, wqT, bq, wkT, bk, wvT, bv, woT, bo,
                                      wrT, rbias, experts, out):
    B, C, T = x.shape
    G = C // P
    NCH = T // CHUNK
    N = B * NCH
    E = wrT.shape[1]
    TB = CHUNK // P
    HD = C // 8
    SCALE = float(HD) ** -0.5
    assert HD == SUB and G == 2 and NCH == 4 and HPG * HD == P and B % 2 == 0

    with ExitStack() as stack:
        def sb(name, shape, dt=F32):
            return stack.enter_context(nc.sbuf_tensor(name, shape, dt))

        def bank(name):
            return stack.enter_context(nc.psum_tensor(name, [P, 512], F32))

        def sem(name):
            return stack.enter_context(nc.semaphore(name))

        x_in = sb("x_in", [P, G, T])
        x_hi = sb("x_hi", [P, G, CHUNK], F32R)
        x_lo = sb("x_lo", [P, G, CHUNK], F32R)
        c_in = sb("c_in", [P, G, CHUNK])
        c_hi = sb("c_hi", [P, G, CHUNK], F32R)
        c_lo = sb("c_lo", [P, G, CHUNK], F32R)
        x_res = sb("x_res", [P, G, CHUNK])
        wq_raw = sb("wq_raw", [P, G, C])
        w_hi = {k: sb(f"w{k}_hi", [P, G, C], F32R) for k in "qkvo"}
        w_lo = {k: sb(f"w{k}_lo", [P, G, C], F32R) for k in "qkvo"}
        bias = {k: sb(f"b{k}_col", [P, G]) for k in "qkvo"}
        keys = sb("keys", [P, G, LEFT + T + LEFT])
        values = sb("values", [P, G, LEFT + T + SUB - LEFT])
        q_diag = sb("q_diag", [P, G, NB, P])
        v_pair = sb("v_pair", [P, G, CHUNK + SUB])
        v_diag = sb("v_diag", [P, G, NB + 1, P])
        v_max = sb("v_max", [P, G, NCH])
        v_top = sb("v_top", [P, G])
        v_unscale = sb("v_unscale", [P, 2, G])
        v_scale = sb("v_scale", [P, G])
        score = sb("score", [P, SCORE_SLOTS, HALF, KEYS])
        prob = sb("prob", [P, 2, HALF, 2 * SUB])
        prob_t = sb("prob_t", [P, G, NB * 2 * SUB])
        att_hi = sb("att_hi", [P, G, CHUNK], F32R)
        att_lo = sb("att_lo", [P, G, CHUNK], F32R)
        x1 = [sb(f"x1_{i}", [P, G, T]) for i in range(2)]
        x1_t = sb("x1_t", [P, G, TB, P])
        ones = x1_t[:, 0, 0, :]
        wr = sb("wr", [P, T // P, E])
        ex = sb("ex", [E + 1, T])
        ident = sb("ident", [P, P])
        ident_b = sb("ident_b", [P, P], BF16)
        mask = sb("mask", [P, HALF, KEYS], BF16)
        wr_sum = sb("wr_sum", [P, E])
        rb = sb("rb", [P, E])
        gates = sb("gates", [P, 2])
        gate_a = sb("gate_a", [P, 1])
        gate_f = sb("gate_f", [P, 1])
        st_in = sb("st_in", [P, G, NCH, 6])
        st_x1 = sb("st_x1", [P, G, NCH, 6])
        mv_in = sb("mv_in", [P, G, 2])
        mv_x1 = sb("mv_x1", [P, G, 2])
        half_var = sb("half_var", [P, G])
        rs_in = sb("rs_in", [P, G])
        rs_x1 = sb("rs_x1", [P, G])
        nt = sb("nt", [P, G])
        pad = sb("pad", [P, 6])
        pool_pad = sb("pool_pad", [P, 1])
        neg_mean_in = sb("neg_mean_in", [P, G])
        neg_mean_x1 = sb("neg_mean_x1", [P, G])
        neg_max = sb("neg_max", [P, UNITS, HALF])
        p_sum = sb("p_sum", [P, UNITS, HALF])
        p_inv = sb("p_inv", [P, UNITS, HALF])
        lg = sb("lg", [P, G, 2, E])
        top = sb("top", [P, G, 8])
        neg_top = sb("neg_top", [P, G])
        z_all = sb("z_all", [P, G, 2])
        z_inv = sb("z_inv", [P, G])
        w_sum = sb("w_sum", [P, G])
        row_a = sb("row_a", [P, G])
        wd = sb("wd", [P, G, E + 1])
        wd_t = sb("wd_t", [E + 1, G, P])

        ps_s = [bank(f"ps_s{i}") for i in range(2)]
        ps_a = [bank(f"ps_a{i}") for i in range(G)]
        ps_j = [bank(f"ps_j{i}") for i in range(2)]
        ps_t = bank("ps_t")
        ps_r = bank("ps_r")

        ctx_in = sem("ctx_in")
        x_ld = [sem(f"x_ld{i}") for i in range(NCH)]
        res_in = sem("res_in")
        out_st = [sem(f"out_st{i}") for i in range(G)]
        w_ld = sem("w_ld")
        consts = sem("consts")
        zeros = sem("zeros")
        w_high = sem("w_high")
        w_low = sem("w_low")
        gate_rdy = sem("gate_rdy")
        sum_mm = sem("sum_mm")
        sum_rdy = sem("sum_rdy")
        av_mm = sem("av_mm")
        s_mm = sem("s_mm")
        o_mm = sem("o_mm")
        q_mm = sem("q_mm")
        v_mm = sem("v_mm")
        k_mm = sem("k_mm")
        t_mm = sem("t_mm")
        r_mm = sem("r_mm")
        wt_mm = sem("wt_mm")
        mix_mm = sem("mix_mm")
        xh_rdy = sem("xh_rdy")
        ch_rdy = sem("ch_rdy")
        xc_rdy = sem("xc_rdy")
        vh_rdy = sem("vh_rdy")
        ph_rdy = sem("ph_rdy")
        ah_rdy = sem("ah_rdy")
        e_rdy = sem("e_rdy")
        q_rdy = sem("q_rdy")
        v_rdy = sem("v_rdy")
        k_rdy = sem("k_rdy")
        xt_rdy = sem("xt_rdy")
        le_rdy = sem("le_rdy")
        wt_rdy = sem("wt_rdy")
        wqh_rdy = sem("wqh_rdy")
        xl_rdy = sem("xl_rdy")
        al_rdy = sem("al_rdy")
        vd_rdy = sem("vd_rdy")
        vm_rdy = sem("vm_rdy")
        vs_rdy = sem("vs_rdy")
        vl_rdy = sem("vl_rdy")
        mx_rdy = sem("mx_rdy")
        sh_rdy = sem("sh_rdy")
        su_rdy = sem("su_rdy")
        iv_rdy = sem("iv_rdy")
        pt_rdy = sem("pt_rdy")
        x1_rdy = sem("x1_rdy")
        st1_rdy = sem("st1_rdy")
        st2_rdy = sem("st2_rdy")
        ln1_rdy = sem("ln1_rdy")
        ln2_rdy = sem("ln2_rdy")
        small = sem("small")
        root1 = sem("root1")
        root2 = sem("root2")
        aggr1 = sem("aggr1")
        aggr2 = sem("aggr2")
        wsum_rdy = sem("wsum_rdy")
        lg_rdy = sem("lg_rdy")
        wd_rdy = sem("wd_rdy")
        wql_rdy = sem("wql_rdy")
        fin_rdy = sem("fin_rdy")
        cl_rdy = sem("cl_rdy")
        pm_rdy = sem("pm_rdy")
        pl_rdy = sem("pl_rdy")

        def done(per, b, c, off, i):
            return b * (per * NCH) + (per * (c + off) + i + 1)

        def live(b, c, off):
            return not isinstance(b, int) or 0 <= NCH * b + c + off < N

        def final(b, g, j):
            return (b + 1) * (NCH * G) + NCH * g + j + 1

        def finishing(b, c):
            if c == 3 and seq(b - 1):
                return 0, 1
            if c == 0 and seq(b - 2):
                return 1, 2
            return None

        def seq(b):
            return not isinstance(b, int) or 0 <= b < B

        def need(eng, s, value):
            if not isinstance(value, int) or value > 0:
                eng.wait_ge(s, value)

        def walk(eng, step):
            for c in (2, 3):
                step(-1, c, 1)
            for b in range(2):
                for c in range(NCH):
                    step(b, c, b % 2)
            with eng.Fori(2, B - 3, 2) as b:
                for c in range(NCH):
                    step(b, c, 0)
                for c in range(NCH):
                    step(b + 1, c, 1)
            for b in range(B - 2, B + 1):
                for c in range(NCH):
                    step(b, c, b % 2)
            step(B + 1, 0, 1 - B % 2)

        def place(c, off):
            return (c + off) % NCH, (c + off) // NCH

        def cols(ch):
            return slice(ch * CHUNK, (ch + 1) * CHUNK)

        def part(words, k):
            v = words.bitcast(F16)
            axes = " ".join(f"a{i}" for i in range(len(v.shape) - 1))
            return v.rearrange(f"{axes} (n k) -> {axes} n k", k=2)[..., k]

        block = stack.enter_context(nc.Block())

        @block.sync
        def _(sp):
            sp.dma_start(x_in[:, :, cols(0)], x[0, :, cols(0)].rearrange("(g p) t -> p g t", g=G)).then_inc(x_ld[0], 16)
            sp.dma_start(c_in[:], ctx[0, :, cols(0)].rearrange("(g p) t -> p g t", g=G)).then_inc(ctx_in, 16)
            for ch in range(1, NCH):
                sp.dma_start(x_in[:, :, cols(ch)],
                             x[0, :, cols(ch)].rearrange("(g p) t -> p g t", g=G)).then_inc(x_ld[ch], 16)
            sp.dma_start(wq_raw[:], wqT.rearrange("(g p) o -> p g o", g=G)).then_inc(w_ld, 16)
            for i, w in enumerate((wkT, wvT, woT)):
                sp.dma_start(x1[1][:, :, i * C:(i + 1) * C], w.rearrange("(g p) o -> p g o", g=G)).then_inc(w_ld, 16)
            for k, v in zip("qkvo", (bq, bk, bv, bo)):
                sp.dma_start(bias[k][:], v).then_inc(w_ld, 16)
            sp.dma_start(gates[:, 0:1], g_xattn.partition_broadcast(P)).then_inc(w_ld, 16)
            sp.dma_start(gates[:, 1:2], g_ffn.partition_broadcast(P)).then_inc(w_ld, 16)
            sp.dma_start(rb[:], rbias.partition_broadcast(P)).then_inc(w_ld, 16)
            sp.dma_start(wr[:], wrT.rearrange("(n p) e -> p n e", p=P)).then_inc(w_ld, 16)
            sp.dma_start(ex[0:E, :], experts).then_inc(w_ld, 16)

            def address(ap):
                if not isinstance(ap.offset, int):
                    sp.to_reg(ap.offset * 4)
                return ap

            def step(b, c, par):
                if live(b, c, 0):
                    rows_in = address(x[b, :, cols(c)].rearrange("(g p) t -> p g t", g=G))
                    need(sp, x1_rdy, done(2, b, c, -1, 1))
                    sp.dma_start(x_res[:], rows_in).then_inc(res_in, 16)
                if finishing(b, c):
                    g, back = finishing(b, c)
                    rows_out = address(out[b - back, g * P:(g + 1) * P, :])
                    need(sp, fin_rdy, final(b - back, g, NCH - 1))
                    sp.dma_start(rows_out, x1[par if back == 2 else 1 - par][:, g, :]).then_inc(out_st[g], 16)
                if live(b, c, 3) and live(b, c, 2):
                    ch, db = place(c, 3)
                    rows_in = address(ctx[b + db, :, cols(ch)].rearrange("(g p) t -> p g t", g=G))
                    need(sp, cl_rdy, done(1, b, c, 2, 0))
                    sp.dma_start(c_in[:], rows_in).then_inc(ctx_in, 16)
                if live(b, c, 5) and live(b, c, 1):
                    ch, db = place(c, 5)
                    rows_in = address(x[b + db, :, cols(ch)].rearrange("(g p) t -> p g t", g=G))
                    need(sp, xl_rdy, done(1, b, c, 1, 0))
                    sp.dma_start(x_in[:, :, cols(ch)], rows_in).then_inc(x_ld[ch], 16)
            walk(sp, step)
            for g in range(G):
                sp.wait_ge(out_st[g], 16 * (B + 1))
            sp.wait_ge(w_ld, 16 * 13)

        @block.gpsimd
        def _(pool):
            pool.memset(keys[:], 0.0).then_inc(zeros, 1)
            pool.memset(values[:], 0.0).then_inc(zeros, 1)
            pool.memset(ident[:], 0.0).then_inc(consts, 1)
            pool.memset(ident_b[:], 0.0).then_inc(consts, 1)
            pool.memset(mask[:], 0.0).then_inc(consts, 1)
            pool.wait_ge(consts, 3)
            pool.affine_select(out=ident[:], in_=ident[:], compare_op=ALU.not_equal, fill=1.0, base=0,
                               pattern=[[-1, P]], channel_multiplier=1).then_inc(consts, 1)
            pool.affine_select(out=ident_b[:], in_=ident_b[:], compare_op=ALU.not_equal, fill=1.0, base=0,
                               pattern=[[-1, P]], channel_multiplier=1).then_inc(consts, 1)
            pool.wait_ge(consts, 5)
            for h in range(HPG):
                m = mask[SUB * h:SUB * (h + 1)]
                pool.affine_select(out=m, in_=m, compare_op=ALU.is_ge, fill=NEG, base=0,
                                   pattern=[[0, HALF], [1, KEYS]], channel_multiplier=-1).then_inc(consts, 1)
                pool.wait_ge(consts, 6 + 2 * h)
                pool.affine_select(out=m, in_=m, compare_op=ALU.is_ge, fill=NEG, base=WINDOW - 1,
                                   pattern=[[0, HALF], [-1, KEYS]], channel_multiplier=1).then_inc(consts, 1)
                pool.wait_ge(consts, 7 + 2 * h)
            pool.memset(ones, 1.0).then_inc(consts, 1)
            pool.memset(q_diag[:], 0.0).then_inc(zeros, 1)
            pool.memset(v_diag[:], 0.0).then_inc(zeros, 1)
            pool.memset(prob[:], 0.0).then_inc(zeros, 1)
            pool.wait_ge(zeros, 5)
            pool.memset(ex[E:E + 1, :], 1.0).then_inc(consts, 1)
            pool.wait_ge(consts, 15)

            NEWTON = 15

            def inverse_root(chain, base, mv, rs, neg_mean, ready):
                k = [0]

                def link(ins):
                    k[0] += 1
                    ins.then_inc(chain, 1)
                    pool.wait_ge(chain, base + k[0])
                    pool.tensor_tensor(pool_pad[:], ident[:, 0:1], ident[:, 0:1], ALU.mult)

                link(pool.tensor_scalar(half_var[:], mv[:, :, 1], EPS, None, ALU.add))
                link(pool.tensor_scalar(rs[:].bitcast(I32), half_var[:].bitcast(I32), -0.5, float(RSQRT_SEED),
                                       ALU.mult, ALU.add))
                link(pool.tensor_scalar(half_var[:], half_var[:], -0.5, None, ALU.mult))
                for _ in range(3):
                    link(pool.tensor_tensor(nt[:], rs[:], rs[:], ALU.mult))
                    link(pool.tensor_tensor(nt[:], nt[:], half_var[:], ALU.mult))
                    link(pool.tensor_scalar(nt[:], nt[:], 1.5, None, ALU.add))
                    link(pool.tensor_tensor(rs[:], rs[:], nt[:], ALU.mult))
                assert k[0] == NEWTON
                pool.tensor_scalar(neg_mean[:], mv[:, :, 0], -1.0, None, ALU.mult).then_inc(ready, 1)

            def ln1(b):
                need(pool, aggr1, (b + 1) * (G + 1))
                pool.tensor_tensor(pool_pad[:], ident[:, 0:1], ident[:, 0:1], ALU.mult)
                inverse_root(root1, b * NEWTON, mv_in, rs_in, neg_mean_in, ln1_rdy)

            ln1(0)

            def step(b, c, par):
                if c == 3 and seq(b + 1) and live(b, c, 0):
                    ln1(b + 1)

                def x_low():
                    ch, _ = place(c, 1)
                    need(pool, xh_rdy, done(1, b, c, 1, 0))
                    pool.tensor_tensor(x_lo[:], x_in[:, :, cols(ch)], x_hi[:], ALU.subtract).then_inc(xl_rdy, 1)

                if live(b, c, 1) and c < 3:
                    x_low()
                if live(b, c, 2):
                    need(pool, ch_rdy, done(1, b, c, 2, 0))
                    pool.tensor_tensor(c_lo[:], c_in[:], c_hi[:], ALU.subtract).then_inc(cl_rdy, 1)
                def normalise(u):
                    need(pool, iv_rdy, done(UNITS, b, c, 0, u))
                    pool.tensor_tensor(score[:, u], score[:, u],
                                       p_inv[:, u, :].unsqueeze(2).to_broadcast([P, HALF, KEYS]),
                                       ALU.mult).then_inc(pm_rdy, 1)

                def low(u):
                    need(pool, ph_rdy, done(UNITS, b, c, 0, u))
                    pool.tensor_tensor(part(prob[:, u % 2], 1)[:, :, 0:KEYS], score[:, u],
                                       part(prob[:, u % 2], 0)[:, :, 0:KEYS], ALU.subtract).then_inc(pl_rdy, 1)

                if live(b, c, 0):
                    normalise(0)
                    normalise(1)
                    low(0)
                    low(1)
                if live(b, c, 1) and c == 3:
                    x_low()
                if live(b, c, 0):
                    normalise(2)
                    normalise(3)
                    low(2)
                    low(3)

                if c == 0 and seq(b - 1):
                    need(pool, aggr2, b * (G + 1))
                    pool.tensor_tensor(pool_pad[:], ident[:, 0:1], ident[:, 0:1], ALU.mult)
                    inverse_root(root2, (b - 1) * NEWTON, mv_x1, rs_x1, neg_mean_x1, ln2_rdy)
            walk(pool, step)

        @block.scalar
        def _(act):
            act.wait_ge(w_ld, 16 * 13)
            act.activation(gate_a[:], gates[:, 0:1], ACT.Tanh).then_inc(gate_rdy, 1)
            act.activation(gate_f[:], gates[:, 1:2], ACT.Tanh).then_inc(gate_rdy, 1)
            act.wait_ge(gate_rdy, 3)
            for i, k in enumerate("kvo"):
                act.activation(w_hi[k][:], x1[1][:, :, i * C:(i + 1) * C], ACT.Copy,
                               ).then_inc(w_high, 1)
            act.wait_ge(zeros, 5)

            def step(b, c, par):
                def attention_high(g):
                    need(act, av_mm, done(2, b, c, -1, g))
                    need(act, o_mm, done(2, b, c, -2, 1))
                    need(act, al_rdy, done(2, b, c, -2, g))
                    act.activation(att_hi[:, g], ps_a[g][:], ACT.Copy,
                                   scale=v_unscale[:, (c - 1) % 2, g:g + 1]).then_inc(ah_rdy, 1)

                def spread_queries(g):
                    need(act, q_mm, done(2, b, c, 0, g))
                    need(act, s_mm, done(UNITS, b, c, -1, UNITS - 1))
                    for h in range(HPG):
                        r = slice(SUB * h, SUB * (h + 1))
                        act.activation(q_diag[r, g, :, r], ps_s[g][r, :].rearrange("p (n i) -> p n i", i=SUB),
                                       ACT.Identity, bias=bias["q"][r, g:g + 1]).then_inc(q_rdy, 1)

                if live(b, c, 0):
                    spread_queries(0)
                if live(b, c, -1):
                    attention_high(0)
                if live(b, c, 0):
                    for g in range(G):
                        if g == 0:
                            need(act, vs_rdy, done(3, b, c, 0, 2))
                        act.activation(part(v_pair[:, g], 0), values[:, g, c * CHUNK:(c + 1) * CHUNK + SUB],
                                       ACT.Copy, scale=v_scale[:, g:g + 1]).then_inc(vh_rdy, 1)
                if live(b, c, -1):
                    attention_high(1)
                if live(b, c, 0):
                    spread_queries(1)

                def centre():
                    ch, db = place(c, 1)
                    need(act, x_ld[ch], (b + db + 1) * 16)
                    need(act, ln1_rdy, b + db + 1)
                    for g in range(G):
                        act.activation(x_in[:, g, cols(ch)], x_in[:, g, cols(ch)], ACT.Identity,
                                       bias=neg_mean_in[:, g:g + 1]).then_inc(xc_rdy, 1)

                def x_high():
                    ch, _ = place(c, 1)
                    need(act, xc_rdy, done(2, b, c, 1, 1))
                    need(act, q_mm, done(2, b, c, 0, 1))
                    act.activation(x_hi[:], x_in[:, :, cols(ch)], ACT.Copy).then_inc(xh_rdy, 1)

                if live(b, c, 1) and c < 3:
                    centre()
                if live(b, c, 1) and c < 3:
                    x_high()
                if live(b, c, 2):
                    need(act, ctx_in, done(1, b, c, 2, 0) * 16)
                    need(act, k_mm, done(2, b, c, 1, 1))
                    need(act, cl_rdy, done(1, b, c, 1, 0))
                    act.activation(c_hi[:], c_in[:], ACT.Copy).then_inc(ch_rdy, 1)
                def exponent(u):
                    need(act, sh_rdy, done(UNITS, b, c, 0, u))
                    act.activation(score[:, u], score[:, u], ACT.Exp, scale=SCALE).then_inc(e_rdy, 1)

                def high(u):
                    need(act, pm_rdy, done(UNITS, b, c, 0, u))
                    need(act, pt_rdy, done(UNITS, b, c, 0, u - 2))
                    act.activation(part(prob[:, u % 2], 0)[:, :, 0:KEYS], score[:, u], ACT.Copy).then_inc(ph_rdy, 1)

                if live(b, c, 0):
                    exponent(0)
                    exponent(1)
                if live(b, c, 1) and c == 3:
                    centre()
                    x_high()
                if c == 2 and seq(b - 1):
                    need(act, wt_mm, b)
                    act.activation(wd_t[:], ps_t[0:E + 1, 0:G * P].rearrange("e (g p) -> e g p", g=G),
                                   ACT.Copy).then_inc(wt_rdy, 1)
                def copy_rows(g):
                    need(act, t_mm, done(2, b, c, -1, g))
                    need(act, r_mm, done(1, b, c, -2, 0))
                    act.activation(x1_t[:, g], ps_t[:].rearrange("p (k t) -> p k t", k=TB), ACT.Copy).then_inc(xt_rdy, 1)

                ch, _ = place(c, 2)
                at = slice(LEFT + ch * CHUNK, LEFT + (ch + 1) * CHUNK)

                def copy_values(g):
                    need(act, v_mm, done(2, b, c, 2, g))
                    need(act, vl_rdy, done(2, b, c, -1, 1))
                    act.activation(values[:, g, at], ps_j[g][:], ACT.Identity,
                                   bias=bias["v"][:, g:g + 1]).then_inc(v_rdy, 1)

                def copy_keys(g):
                    need(act, k_mm, done(2, b, c, 2, g))
                    need(act, s_mm, done(UNITS, b, c, -1, UNITS - 1))
                    act.activation(keys[:, g, at], ps_j[g][:], ACT.Identity,
                                   bias=bias["k"][:, g:g + 1]).then_inc(k_rdy, 1)

                if live(b, c, 0):
                    exponent(2)
                    high(0)
                if live(b, c, -1):
                    copy_rows(0)
                if live(b, c, 2):
                    copy_values(0)
                if live(b, c, 0):
                    exponent(3)
                    high(1)
                if live(b, c, 2):
                    copy_values(1)
                if c == 1 and seq(b - 1):
                    need(act, lg_rdy, b * G)
                    for g in range(G):
                        for j in range(2):
                            act.activation(lg[:, g, j], lg[:, g, j], ACT.Exp, bias=neg_top[:, g:g + 1],
                                           accum_out=z_all[:, g, j:j + 1]).then_inc(le_rdy, 1)
                if c == 3 and seq(b + 1):
                    need(act, ln1_rdy, b + 2)
                    need(act, q_mm, done(2, b, c, 0, 1))
                    for g in range(G):
                        act.activation(w_hi["q"][:, g], wq_raw[:, g], ACT.Copy, scale=rs_in[:, g:g + 1]).then_inc(wqh_rdy, 1)
                if live(b, c, -1):
                    copy_rows(1)
                if live(b, c, 2):
                    copy_keys(0)
                if live(b, c, 0):
                    high(2)
                if live(b, c, 2):
                    copy_keys(1)
                if live(b, c, 0):
                    high(3)

            walk(act, step)

        @block.vector
        def _(dve):
            dve.wait_ge(gate_rdy, 2)
            dve.wait_ge(w_ld, 16 * 13)
            wo_staged = x1[1][:, :, 2 * C:3 * C]
            dve.tensor_scalar(wo_staged, wo_staged, gate_a[:], None, ALU.mult).then_inc(gate_rdy, 1)
            dve.tensor_scalar(bias["o"][:], bias["o"][:], gate_a[:], None, ALU.mult).then_inc(sum_rdy, 1)
            for i, k in enumerate("kvo"):
                dve.wait_ge(w_high, i + 1)
                dve.tensor_tensor(w_lo[k][:], x1[1][:, :, i * C:(i + 1) * C], w_hi[k][:], ALU.subtract).then_inc(w_low, 1)
            dve.wait_ge(sum_mm, 1)
            dve.tensor_copy(wr_sum[:], ps_r[:, 0:E]).then_inc(sum_rdy, 1)
            dve.memset(pad[:, 3:4], 0.0).then_inc(fin_rdy, NCH * G)
            for g in range(G):
                dve.memset(pad[:, 4 + g:5 + g], 0.0).then_inc(out_st[g], 16)

            dve.wait_ge(sum_rdy, 2)
            dve.wait_ge(zeros, 5)

            def stats_in(g, ch):
                dve.bn_stats(st_in[:, g, ch], x_in[:, g, cols(ch)]).then_inc(st1_rdy, 1)

            def aggregate_in(b):
                need(dve, st1_rdy, b * (NCH * G) + NCH * G)
                dve.memset(pad[:, 1:2], 0.0).then_inc(aggr1, 1)
                for g in range(G):
                    dve.bn_aggr(mv_in[:, g], st_in[:, g]).then_inc(aggr1, 1)

            for ch in range(NCH):
                dve.wait_ge(x_ld[ch], 16)
                for g in range(G):
                    stats_in(g, ch)
            aggregate_in(0)
            ROUTER = 12

            def step(b, c, par):
                def attention_low(g):
                    need(dve, ah_rdy, done(2, b, c, -1, g))
                    dve.scalar_tensor_tensor(att_lo[:, g], ps_a[g][:], v_unscale[:, (c - 1) % 2, g:g + 1],
                                             att_hi[:, g], ALU.mult, ALU.subtract).then_inc(al_rdy, 1)

                def values_low(g):
                    need(dve, vh_rdy, done(2, b, c, 0, g))
                    dve.scalar_tensor_tensor(part(v_pair[:, g], 1), values[:, g, c * CHUNK:(c + 1) * CHUNK + SUB],
                                             v_scale[:, g:g + 1], part(v_pair[:, g], 0),
                                             ALU.mult, ALU.subtract).then_inc(vl_rdy, 1)

                def spread(g, heads):
                    need(dve, vl_rdy, done(2, b, c, 0, g))
                    need(dve, av_mm, done(2, b, c, -1, g))
                    for h in heads:
                        r = slice(SUB * h, SUB * (h + 1))
                        dve.transpose(v_diag[r, g, :, r],
                                      v_pair[r, g].rearrange("p (n i) -> p n i", i=SUB)).then_inc(vd_rdy, 1)

                def scores_of(u):
                    return ps_s[u % 2][:, 0:HALF * KEYS].rearrange("p (n k) -> p n k", k=KEYS)

                def largest(u):
                    need(dve, s_mm, done(UNITS, b, c, 0, u))
                    dve.tensor_reduce(neg_max[:, u], scores_of(u), AX, ALU.max, negate=True).then_inc(mx_rdy, 1)

                def shift(u):
                    need(dve, mx_rdy, done(UNITS, b, c, 0, u))
                    need(dve, pl_rdy, done(UNITS, b, c, 0, u - SCORE_SLOTS))
                    dve.tensor_tensor(score[:, u], scores_of(u), neg_max[:, u, :].unsqueeze(2).to_broadcast([P, HALF, KEYS]),
                                      ALU.add).then_inc(sh_rdy, 1)

                def total(u):
                    need(dve, e_rdy, done(UNITS, b, c, 0, u))
                    dve.tensor_reduce(p_sum[:, u], score[:, u], AX, ALU.add).then_inc(su_rdy, 1)

                def invert(u):
                    need(dve, su_rdy, done(UNITS, b, c, 0, u))
                    dve.reciprocal(p_inv[:, u], p_sum[:, u]).then_inc(iv_rdy, 1)

                def turn(u):
                    need(dve, pl_rdy, done(UNITS, b, c, 0, u))
                    need(dve, av_mm, done(2, b, c, -1, u // 2))
                    dve.transpose(prob_t[:, u // 2, (u % 2) * CHUNK:(u % 2 + 1) * CHUNK],
                                  prob[:, u % 2].rearrange("p n k -> p (n k)")).then_inc(pt_rdy, 1)

                def residual(g):
                    ch, db = place(c, -1)
                    buf = x1[(par if db == 0 else 1 - par)]
                    need(dve, o_mm, done(2, b, c, -1, g))
                    need(dve, res_in, done(1, b, c, -1, 0) * 16)
                    if ch == 0:
                        need(dve, out_st[g], b * 16)
                    dve.scalar_tensor_tensor(buf[:, g, cols(ch)], ps_j[g][:], bias["o"][:, g:g + 1], x_res[:, g],
                                             ALU.add, ALU.add).then_inc(x1_rdy, 1)

                def stats_x1(g):
                    ch, db = place(c, -1)
                    buf = x1[(par if db == 0 else 1 - par)]
                    need(dve, x1_rdy, done(2, b, c, -1, g))
                    dve.bn_stats(st_x1[:, g, ch], buf[:, g, cols(ch)]).then_inc(st2_rdy, 1)

                def finish(g, back, j):
                    buf = x1[par if back == 2 else 1 - par]
                    need(dve, mix_mm, (b - back) * (NCH * G) + NCH * g + j + 1)
                    dve.scalar_tensor_tensor(buf[:, g, cols(j)], buf[:, g, cols(j)], row_a[:, g:g + 1],
                                             ps_j[j % 2][:], ALU.mult, ALU.add).then_inc(fin_rdy, 1)

                def values_largest():
                    ch, _ = place(c, 2)
                    need(dve, v_rdy, done(2, b, c, 2, 1))
                    dve.tensor_reduce(v_max[:, :, ch], values[:, :, LEFT + ch * CHUNK:LEFT + (ch + 1) * CHUNK],
                                      AX, ALU.max, apply_absolute_value=True).then_inc(vm_rdy, 1)

                def values_scale(stage):
                    ch, _ = place(c, 1)
                    first, last = max(ch - 1, 0), min(ch + 1, NCH - 1)
                    slot = v_unscale[:, ch % 2]
                    if stage == 0:
                        need(dve, vm_rdy, done(1, b, c, 2 if live(b, c, 2) else 1, 0))
                        dve.tensor_reduce(v_top[:], v_max[:, :, first:last + 1], AX, ALU.max).then_inc(vs_rdy, 1)
                    if stage == 1:
                        need(dve, vs_rdy, done(3, b, c, 1, 0))
                        dve.tensor_scalar(slot, v_top[:], TINY, 1.0 / TOP, ALU.max, ALU.mult).then_inc(vs_rdy, 1)
                    if stage == 2:
                        need(dve, vs_rdy, done(3, b, c, 1, 1))
                        dve.reciprocal(v_scale[:], slot).then_inc(vs_rdy, 1)

                now, before, stats = live(b, c, 0), live(b, c, -1), live(b, c, 4) and live(b, c, 0)
                if stats:
                    ch, db = place(c, 4)
                    need(dve, x_ld[ch], (b + db + 1) * 16)
                    stats_in(0, ch)
                if before:
                    attention_low(0)
                if now:
                    largest(0)
                if stats:
                    stats_in(1, ch)
                if now:
                    shift(0)
                    values_low(0)
                if stats and c == 3:
                    aggregate_in(b + 1)
                if finishing(b, c):
                    finish(*finishing(b, c), 0)
                    finish(*finishing(b, c), 1)
                if before:
                    attention_low(1)
                if finishing(b, c):
                    finish(*finishing(b, c), 2)
                    finish(*finishing(b, c), 3)
                if now:
                    spread(0, range(HPG))
                if before:
                    residual(0)
                if now:
                    largest(1)
                if before:
                    stats_x1(0)
                if now:
                    shift(1)
                if before:
                    residual(1)
                if now:
                    total(0)
                    largest(2)
                    invert(0)
                    shift(2)
                if before:
                    stats_x1(1)
                if c == 0 and seq(b - 1):
                    need(dve, st2_rdy, b * (NCH * G))
                    dve.memset(pad[:, 2:3], 0.0).then_inc(aggr2, 1)
                    for g in range(G):
                        dve.bn_aggr(mv_x1[:, g], st_x1[:, g]).then_inc(aggr2, 1)
                if now:
                    total(1)
                    largest(3)
                    invert(1)
                    shift(3)
                if c == 1 and seq(b - 1):
                    router_logits(b)
                if now:
                    total(2)
                    turn(0)
                    invert(2)
                    total(3)
                    turn(1)
                    invert(3)
                    values_low(1)
                if c == 3 and seq(b + 1):
                    need(dve, wqh_rdy, (b + 2) * G)
                    for g in range(G):
                        dve.scalar_tensor_tensor(w_lo["q"][:, g], wq_raw[:, g], rs_in[:, g:g + 1], w_hi["q"][:, g],
                                                 ALU.mult, ALU.subtract).then_inc(wql_rdy, 1)
                if live(b, c, 2):
                    values_largest()
                if now:
                    spread(1, (0, 1))
                if live(b, c, 1):
                    values_scale(0)
                if now:
                    spread(1, (2,))
                if live(b, c, 1):
                    values_scale(1)
                if now:
                    spread(1, (3,))
                if live(b, c, 1):
                    values_scale(2)
                if c == 1 and seq(b - 1):
                    router_weights(b)
                if now:
                    turn(2)
                    turn(3)

            def router_logits(b):
                base = (b - 1) * ROUTER
                need(dve, r_mm, (b - 1) * NCH + NCH)
                need(dve, ln2_rdy, b)
                for g in range(G):
                    dve.scalar_tensor_tensor(wd[:, g, 0:E], wr_sum[:], neg_mean_x1[:, g:g + 1], ps_r[:, g * E:(g + 1) * E],
                                             ALU.mult, ALU.add).then_inc(small, 1)
                dve.wait_ge(small, base + 2)
                for g in range(G):
                    dve.scalar_tensor_tensor(lg[:, g, 0], wd[:, g, 0:E], rs_x1[:, g:g + 1], rb[:],
                                             ALU.mult, ALU.add).then_inc(small, 1)
                dve.wait_ge(small, base + 4)
                dve.memset(pad[:, 0:1], 0.0).then_inc(small, 1)
                for g in range(G):
                    dve.max(top[:, g], lg[:, g, 0]).then_inc(small, 1)
                dve.wait_ge(small, base + 7)
                dve.tensor_scalar(neg_top[:], top[:, :, 0], -1.0, None, ALU.mult).then_inc(small, 1)
                dve.match_replace(lg[:, 0, 1], top[:, 0], lg[:, 0, 0], NEG).then_inc(lg_rdy, 1)
                dve.match_replace(lg[:, 1, 1], top[:, 1], lg[:, 1, 0], NEG).then_inc(lg_rdy, 1)

            def router_weights(b):
                base = (b - 1) * ROUTER
                need(dve, le_rdy, b * (2 * G))
                need(dve, lg_rdy, b * G)
                dve.reciprocal(z_inv[:], z_all[:, :, 0]).then_inc(small, 1)
                dve.tensor_tensor(wd[:, :, 0:E], lg[:, :, 0], lg[:, :, 1], ALU.subtract).then_inc(small, 1)
                dve.wait_ge(small, base + 10)
                dve.tensor_scalar(z_inv[:], z_inv[:], gate_f[:], None, ALU.mult).then_inc(small, 1)
                dve.wait_ge(small, base + 11)
                dve.tensor_tensor(wd[:, :, 0:E], wd[:, :, 0:E], z_inv[:].unsqueeze(2).to_broadcast([P, G, E]),
                                  ALU.mult).then_inc(small, 1)
                dve.wait_ge(small, base + 12)
                dve.tensor_reduce(w_sum[:], wd[:, :, 0:E], AX, ALU.add).then_inc(wsum_rdy, 1)
                need(dve, wsum_rdy, 3 * b - 2)
                dve.tensor_tensor(w_sum[:], w_sum[:], rs_x1[:], ALU.mult).then_inc(wsum_rdy, 1)
                need(dve, wsum_rdy, 3 * b - 1)
                dve.tensor_scalar(row_a[:], w_sum[:], 1.0, None, ALU.add).then_inc(wsum_rdy, 1)
                dve.tensor_tensor(wd[:, :, E:E + 1].rearrange("p g o -> p (g o)"), w_sum[:], neg_mean_x1[:],
                                  ALU.mult).then_inc(wd_rdy, 1)

            walk(dve, step)

        @block.tensor
        def _(pe):
            pe.wait_ge(w_ld, 16 * 13)
            pe.wait_ge(consts, 15)
            for i in range(T // P):
                ins = pe.matmul(ps_r[:, 0:E], ones, wr[:, i], start=(i == 0), stop=(i == T // P - 1))
            ins.then_inc(sum_mm, 1)
            pe.wait_ge(w_low, 3)

            def project(dst, k, g, hi, lo):
                o = slice(g * P, (g + 1) * P)
                terms = [(w_hi[k], hi), (w_lo[k], hi), (w_hi[k], lo)]
                n = 0
                for w, v in terms:
                    for i in range(G):
                        ins = pe.matmul(dst[:], w[:, i, o], v[:, i], start=(n == 0), stop=(n == 2 * G + 1))
                        n += 1
                return ins

            def step(b, c, par):
                def mixture(g, back, j):
                    need(pe, wt_rdy, b - back + 1)
                    if j < 2 and live(b, c, 1):
                        need(pe, k_rdy, done(2, b, c, 1, j))
                    elif j < 2 and live(b, c, -2):
                        need(pe, x1_rdy, done(2, b, c, -2, j))
                    elif j < 2:
                        need(pe, x1_rdy, 2 * N)
                        need(pe, fin_rdy, final(B - 1, g - 1, 2 + j))
                    else:
                        need(pe, fin_rdy, final(b - back, g, j - 2))
                    pe.matmul(ps_j[j % 2][:], wd_t[:, g], ex[:, cols(j)], start=True, stop=True).then_inc(mix_mm, 1)

                if live(b, c, 0):
                    for g in range(G):
                        need(pe, xl_rdy, done(1, b, c, 0, 0))
                        need(pe, wql_rdy, (b + 1) * G)
                        need(pe, sh_rdy, done(UNITS, b, c, -1, 2 + g))
                        project(ps_s[g], "q", g, x_hi, x_lo).then_inc(q_mm, 1)
                def scores(u):
                    g, half = u // 2, u % 2
                    if u < 2:
                        need(pe, q_rdy, done(8, b, c, 0, 4 * u + 3))
                    else:
                        need(pe, sh_rdy, done(UNITS, b, c, 0, u - 2))
                    s = ps_s[u % 2]
                    pe.matmul(s[:, 0:HALF * KEYS], ident_b[:], mask[:].rearrange("p n k -> p (n k)"),
                              start=True, stop=False)
                    for n in range(HALF):
                        tb = half * HALF + n
                        at = c * CHUNK + tb * SUB
                        ins = pe.matmul(s[:, n * KEYS:(n + 1) * KEYS], q_diag[:, g, tb], keys[:, g, at:at + KEYS],
                                        start=False, stop=(n == HALF - 1))
                    ins.then_inc(s_mm, 1)

                def output(g):
                    if g == 0:
                        need(pe, al_rdy, done(2, b, c, -1, 1))
                    if live(b, c, 1):
                        need(pe, k_rdy, done(2, b, c, 1, g))
                    if c == 3 and seq(b - 1):
                        need(pe, fin_rdy, final(b - 1, 0, 2 + g))
                    if c == 0 and seq(b - 2):
                        need(pe, fin_rdy, final(b - 2, 1, 2 + g))
                    project(ps_j[g], "o", g, att_hi, att_lo).then_inc(o_mm, 1)

                def attend(g):
                    need(pe, pt_rdy, done(UNITS, b, c, -1, 2 * g + 1))
                    need(pe, vd_rdy, done(8, b, c, -1, 4 * g + 3))
                    need(pe, al_rdy, done(2, b, c, -2, g))
                    for j in range(NB + 1):
                        lo = max(0, (2 * j - 1) * SUB)
                        hi = min(2 * NB * SUB, (2 * j + 1) * SUB)
                        q0 = max(0, (j - 1) * SUB)
                        q1 = min(CHUNK, (j + 1) * SUB)
                        for n, (kv, kp) in enumerate(((0, 0), (1, 0), (0, 1))):
                            ins = pe.matmul(ps_a[g][:, q0:q1], part(v_diag[:, g, j], kv),
                                            part(prob_t[:, g, lo:hi], kp),
                                            start=(j == 0 and n == 0), stop=(j == NB), skip_group_check=True)
                    ins.then_inc(av_mm, 1)

                if live(b, c, -1):
                    attend(0)
                if live(b, c, 0):
                    need(pe, k_rdy, done(2, b, c, 1 if live(b, c, 1) else 0, 1))
                    scores(0)
                if finishing(b, c):
                    for j in (0, 1):
                        mixture(*finishing(b, c), j)
                if live(b, c, -1):
                    attend(1)
                if finishing(b, c):
                    for j in (2, 3):
                        mixture(*finishing(b, c), j)
                if live(b, c, -1):
                    output(0)
                if live(b, c, 0):
                    scores(1)
                if live(b, c, -1):
                    output(1)
                if c == 2 and seq(b - 1):
                    need(pe, wd_rdy, b)
                    need(pe, xt_rdy, done(2, b, c, -2, 1) if live(b, c, -2) else 2 * N)
                    for g in range(G):
                        ins = pe.transpose(ps_t[0:E + 1, g * P:(g + 1) * P], wd[:, g], ident[:])
                    ins.then_inc(wt_mm, 1)
                def rows(g):
                    ch, db = place(c, -1)
                    buf = x1[(par if db == 0 else 1 - par)]
                    need(pe, x1_rdy, done(2, b, c, -1, g))
                    need(pe, xt_rdy, done(2, b, c, -1, g - 1))
                    if c == 2 and seq(b - 1):
                        need(pe, wt_rdy, b)
                    for k in range(TB):
                        t = ch * CHUNK + k * P
                        ins = pe.transpose(ps_t[:, k * P:(k + 1) * P], buf[:, g, t:t + P], ident[:])
                    ins.then_inc(t_mm, 1)

                if live(b, c, 0):
                    scores(2)
                if live(b, c, -1):
                    rows(0)
                if live(b, c, 0):
                    scores(3)
                if live(b, c, 2):
                    for g in range(G):
                        need(pe, cl_rdy, done(1, b, c, 2, 0))
                        if live(b, c, -1):
                            need(pe, x1_rdy, done(2, b, c, -1, g))
                        else:
                            need(pe, k_rdy, done(2, b, c, 1, g))
                        project(ps_j[g], "v", g, c_hi, c_lo).then_inc(v_mm, 1)
                if live(b, c, -1):
                    rows(1)
                if live(b, c, 2):
                    for g in range(G):
                        need(pe, v_rdy, done(2, b, c, 2, g))
                        project(ps_j[g], "k", g, c_hi, c_lo).then_inc(k_mm, 1)
                if live(b, c, -1):
                    ch, db = place(c, -1)
                    need(pe, xt_rdy, done(2, b, c, -1, 1))
                    if ch == 0:
                        need(pe, lg_rdy, b * G)
                        if isinstance(b, int) and b == 0:
                            need(pe, sum_rdy, 2)
                    for k in range(TB):
                        for g in range(G):
                            ins = pe.matmul(ps_r[:, g * E:(g + 1) * E], x1_t[:, g, k], wr[:, ch * TB + k],
                                            start=(ch == 0 and k == 0 and g == 0),
                                            stop=(ch == NCH - 1 and k == TB - 1), skip_group_check=True)
                    ins.then_inc(r_mm, 1)
            walk(pe, step)


def kernel(**inputs):
    import numpy as np
    import concourse.bacc as bacc
    from concourse import mybir as _mybir
    from concourse.bass_utils import run_bass_kernel_spmd as run

    a = {k: np.asarray(v) for k, v in inputs.items()}
    col = lambda v: np.ascontiguousarray(v.reshape(2, 128).T)
    arrays = {
        "x_dram": a["x"], "ctx_dram": a["ctx_4096"], "g_xattn_dram": a["g_xattn"], "g_ffn_dram": a["g_ffn"],
        "wqT_dram": a["L0_xattn_Wq"].T, "bq_dram": col(a["L0_xattn_bq"]),
        "wkT_dram": a["L0_xattn_Wk"].T, "bk_dram": col(a["L0_xattn_bk"]),
        "wvT_dram": a["L0_xattn_Wv"].T, "bv_dram": col(a["L0_xattn_bv"]),
        "woT_dram": a["L0_xattn_Wo"].T, "bo_dram": col(a["L0_xattn_bo"]),
        "wrT_dram": a["L0_ffn_router_weight"].T, "rbias_dram": a["L0_ffn_router_bias"],
        "experts_dram": a["L0_ffn_expert_bias"],
    }
    arrays = {k: np.ascontiguousarray(v) for k, v in arrays.items()}
    nc = bacc.Bacc("TRN2", target_bir_lowering=False, num_devices=1)
    args = [nc.dram_tensor(k, v.shape, _mybir.dt.from_np(v.dtype), kind="ExternalInput").ap() for k, v in arrays.items()]
    args.append(nc.dram_tensor("out_dram", a["x"].shape, _mybir.dt.float32, kind="ExternalOutput").ap())
    gated_window_attention_and_router(nc, *args)
    r = run(nc, [arrays], core_ids=[0])
    return r.results[0]["out_dram"]
```

```python
from contextlib import ExitStack

import concourse.bass as bass
from concourse import mybir

F32 = mybir.dt.float32
F32R = mybir.dt.float32r
BF16 = mybir.dt.bfloat16
F16 = mybir.dt.float16
I32 = mybir.dt.int32
ALU = mybir.AluOpType
ACT = mybir.ActivationFunctionType
AX = mybir.AxisListType.X

P = 128
SUB = 32
HPG = 4
WINDOW = 16
LEFT = WINDOW // 2
KEYS = 48
CHUNK = 512
NB = CHUNK // SUB
HALF = NB // 2
UNITS = 4
EPS = 1e-5
NEG = -1e30
RSQRT_SEED = 0x5F3759DF
SCORE_SLOTS = 4
TOP = 2.0 ** 14
TINY = 1e-30


def gated_window_attention_and_router(nc, x, ctx, g_xattn, g_ffn, wqT, bq, wkT, bk, wvT, bv, woT, bo,
                                      wrT, rbias, experts, out):
    B, C, T = x.shape
    G = C // P
    NCH = T // CHUNK
    N = B * NCH
    E = wrT.shape[1]
    TB = CHUNK // P
    HD = C // 8
    SCALE = float(HD) ** -0.5
    assert HD == SUB and G == 2 and NCH == 4 and HPG * HD == P and B % 2 == 0

    with ExitStack() as stack:
        def sb(name, shape, dt=F32):
            return stack.enter_context(nc.sbuf_tensor(name, shape, dt))

        def bank(name):
            return stack.enter_context(nc.psum_tensor(name, [P, 512], F32))

        def sem(name):
            return stack.enter_context(nc.semaphore(name))

        x_in = sb("x_in", [P, G, T])
        x_hi = sb("x_hi", [P, G, CHUNK], F32R)
        x_lo = sb("x_lo", [P, G, CHUNK], F32R)
        c_in = sb("c_in", [P, G, CHUNK])
        c_hi = sb("c_hi", [P, G, CHUNK], F32R)
        c_lo = sb("c_lo", [P, G, CHUNK], F32R)
        x_res = sb("x_res", [P, G, CHUNK])
        wq_raw = sb("wq_raw", [P, G, C])
        w_hi = {k: sb(f"w{k}_hi", [P, G, C], F32R) for k in "qkvo"}
        w_lo = {k: sb(f"w{k}_lo", [P, G, C], F32R) for k in "qkvo"}
        bias = {k: sb(f"b{k}_col", [P, G]) for k in "qkvo"}
        keys = sb("keys", [P, G, LEFT + T + LEFT])
        values = sb("values", [P, G, LEFT + T + SUB - LEFT])
        q_diag = sb("q_diag", [P, G, NB, P])
        v_pair = sb("v_pair", [P, G, CHUNK + SUB])
        v_diag = sb("v_diag", [P, G, NB + 1, P])
        v_max = sb("v_max", [P, G, NCH])
        v_top = sb("v_top", [P, G])
        v_unscale = sb("v_unscale", [P, 2, G])
        v_scale = sb("v_scale", [P, G])
        score = sb("score", [P, SCORE_SLOTS, HALF, KEYS])
        prob = sb("prob", [P, 2, HALF, 2 * SUB])
        prob_t = sb("prob_t", [P, G, NB * 2 * SUB])
        att_hi = sb("att_hi", [P, G, CHUNK], F32R)
        att_lo = sb("att_lo", [P, G, CHUNK], F32R)
        x1 = [sb(f"x1_{i}", [P, G, T]) for i in range(2)]
        x1_t = sb("x1_t", [P, G, TB, P])
        ones = x1_t[:, 0, 0, :]
        wr = sb("wr", [P, T // P, E])
        ex = sb("ex", [E + 1, T])
        ident = sb("ident", [P, P])
        ident_b = sb("ident_b", [P, P], BF16)
        mask = sb("mask", [P, HALF, KEYS], BF16)
        wr_sum = sb("wr_sum", [P, E])
        rb = sb("rb", [P, E])
        gates = sb("gates", [P, 2])
        gate_a = sb("gate_a", [P, 1])
        gate_f = sb("gate_f", [P, 1])
        st_in = sb("st_in", [P, G, NCH, 6])
        st_x1 = sb("st_x1", [P, G, NCH, 6])
        mv_in = sb("mv_in", [P, G, 2])
        mv_x1 = sb("mv_x1", [P, G, 2])
        half_var = sb("half_var", [P, G])
        rs_in = sb("rs_in", [P, G])
        rs_x1 = sb("rs_x1", [P, G])
        nt = sb("nt", [P, G])
        pad = sb("pad", [P, 6])
        pool_pad = sb("pool_pad", [P, 1])
        neg_mean_in = sb("neg_mean_in", [P, G])
        neg_mean_x1 = sb("neg_mean_x1", [P, G])
        neg_max = sb("neg_max", [P, UNITS, HALF])
        p_sum = sb("p_sum", [P, UNITS, HALF])
        p_inv = sb("p_inv", [P, UNITS, HALF])
        lg = sb("lg", [P, G, 2, E])
        top = sb("top", [P, G, 8])
        neg_top = sb("neg_top", [P, G])
        z_all = sb("z_all", [P, G, 2])
        z_inv = sb("z_inv", [P, G])
        w_sum = sb("w_sum", [P, G])
        row_a = sb("row_a", [P, G])
        wd = sb("wd", [P, G, E + 1])
        wd_t = sb("wd_t", [E + 1, G, P])

        ps_s = [bank(f"ps_s{i}") for i in range(2)]
        ps_a = [bank(f"ps_a{i}") for i in range(G)]
        ps_j = [bank(f"ps_j{i}") for i in range(2)]
        ps_t = bank("ps_t")
        ps_r = bank("ps_r")

        ctx_in = sem("ctx_in")
        x_ld = [sem(f"x_ld{i}") for i in range(NCH)]
        res_in = sem("res_in")
        out_st = [sem(f"out_st{i}") for i in range(G)]
        w_ld = sem("w_ld")
        r_ld = sem("r_ld")
        consts = sem("consts")
        zeros = sem("zeros")
        w_high = sem("w_high")
        w_low = sem("w_low")
        gate_rdy = sem("gate_rdy")
        sum_mm = sem("sum_mm")
        sum_rdy = sem("sum_rdy")
        av_mm = sem("av_mm")
        s_mm = sem("s_mm")
        o_mm = sem("o_mm")
        q_mm = sem("q_mm")
        v_mm = sem("v_mm")
        k_mm = sem("k_mm")
        t_mm = sem("t_mm")
        r_mm = sem("r_mm")
        wt_mm = sem("wt_mm")
        mix_mm = sem("mix_mm")
        xh_rdy = sem("xh_rdy")
        ch_rdy = sem("ch_rdy")
        xc_rdy = sem("xc_rdy")
        vh_rdy = sem("vh_rdy")
        ph_rdy = sem("ph_rdy")
        ah_rdy = sem("ah_rdy")
        e_rdy = sem("e_rdy")
        q_rdy = sem("q_rdy")
        v_rdy = sem("v_rdy")
        k_rdy = sem("k_rdy")
        xt_rdy = sem("xt_rdy")
        le_rdy = sem("le_rdy")
        wt_rdy = sem("wt_rdy")
        wqh_rdy = sem("wqh_rdy")
        ob_rdy = sem("ob_rdy")
        xl_rdy = sem("xl_rdy")
        al_rdy = sem("al_rdy")
        vd_rdy = sem("vd_rdy")
        vm_rdy = sem("vm_rdy")
        vs_rdy = sem("vs_rdy")
        vl_rdy = sem("vl_rdy")
        mx_rdy = sem("mx_rdy")
        sh_rdy = sem("sh_rdy")
        su_rdy = sem("su_rdy")
        iv_rdy = sem("iv_rdy")
        pt_rdy = sem("pt_rdy")
        x1_rdy = [sem(f"x1_rdy{g}") for g in range(G)]
        st1_rdy = sem("st1_rdy")
        st2_rdy = sem("st2_rdy")
        ln1_rdy = sem("ln1_rdy")
        ln2_rdy = sem("ln2_rdy")
        small = sem("small")
        root1 = sem("root1")
        root2 = sem("root2")
        aggr1 = sem("aggr1")
        aggr2 = sem("aggr2")
        wsum_rdy = sem("wsum_rdy")
        lg_rdy = sem("lg_rdy")
        wd_rdy = sem("wd_rdy")
        wql_rdy = sem("wql_rdy")
        fin_rdy = sem("fin_rdy")
        cl_rdy = sem("cl_rdy")
        pm_rdy = sem("pm_rdy")
        pl_rdy = sem("pl_rdy")

        def done(per, b, c, off, i):
            return b * (per * NCH) + (per * (c + off) + i + 1)

        def live(b, c, off):
            return not isinstance(b, int) or 0 <= NCH * b + c + off < N

        def final(b, g, j):
            return (b + 1) * (NCH * G) + NCH * g + j + 1

        def finishing(b, c):
            return c >= 2 and seq(b - 1)

        def seq(b):
            return not isinstance(b, int) or 0 <= b < B

        def need(eng, s, value):
            if not isinstance(value, int) or value > 0:
                eng.wait_ge(s, value)

        def walk(eng, step):
            for c in (2, 3):
                step(-1, c, 1)
            for b in range(2):
                for c in range(NCH):
                    step(b, c, b % 2)
            with eng.Fori(2, B - 3, 2) as b:
                for c in range(NCH):
                    step(b, c, 0)
                for c in range(NCH):
                    step(b + 1, c, 1)
            for b in range(B - 2, B + 1):
                for c in range(NCH):
                    step(b, c, b % 2)

        def place(c, off):
            return (c + off) % NCH, (c + off) // NCH

        def cols(ch):
            return slice(ch * CHUNK, (ch + 1) * CHUNK)

        def part(words, k):
            v = words.bitcast(F16)
            axes = " ".join(f"a{i}" for i in range(len(v.shape) - 1))
            return v.rearrange(f"{axes} (n k) -> {axes} n k", k=2)[..., k]

        block = stack.enter_context(nc.Block())

        @block.sync
        def _(sp):
            sp.dma_start(c_in[:], ctx[0, :, cols(0)].rearrange("(g p) t -> p g t", g=G)).then_inc(ctx_in, 16)
            for i, w in enumerate((wkT, wvT, woT)):
                sp.dma_start(x1[1][:, :, i * C:(i + 1) * C], w.rearrange("(g p) o -> p g o", g=G)).then_inc(w_ld, 16)
            sp.dma_start(wq_raw[:], wqT.rearrange("(g p) o -> p g o", g=G)).then_inc(w_ld, 16)
            for k, v in zip("qkvo", (bq, bk, bv, bo)):
                sp.dma_start(bias[k][:], v).then_inc(w_ld, 16)
            sp.dma_start(gates[:, 0:1], g_xattn.partition_broadcast(P)).then_inc(w_ld, 16)
            sp.dma_start(gates[:, 1:2], g_ffn.partition_broadcast(P)).then_inc(w_ld, 16)
            for ch in range(NCH):
                sp.dma_start(x_in[:, :, cols(ch)],
                             x[0, :, cols(ch)].rearrange("(g p) t -> p g t", g=G)).then_inc(x_ld[ch], 16)
            sp.dma_start(rb[:], rbias.partition_broadcast(P)).then_inc(r_ld, 16)
            sp.dma_start(wr[:], wrT.rearrange("(n p) e -> p n e", p=P)).then_inc(r_ld, 16)
            sp.dma_start(ex[0:E, :], experts).then_inc(r_ld, 16)

            def address(ap):
                if not isinstance(ap.offset, int):
                    sp.to_reg(ap.offset * 4)
                return ap

            def step(b, c, par):
                if live(b, c, 0):
                    rows_in = address(x[b, :, cols(c)].rearrange("(g p) t -> p g t", g=G))
                    for g in range(G):
                        need(sp, x1_rdy[g], done(1, b, c, -1, 0))
                    sp.dma_start(x_res[:], rows_in).then_inc(res_in, 16)
                if live(b, c, 3) and live(b, c, 2):
                    ch, db = place(c, 3)
                    rows_in = address(ctx[b + db, :, cols(ch)].rearrange("(g p) t -> p g t", g=G))
                    need(sp, cl_rdy, done(1, b, c, 2, 0))
                    sp.dma_start(c_in[:], rows_in).then_inc(ctx_in, 16)
                if live(b, c, 5) and live(b, c, 1):
                    ch, db = place(c, 5)
                    rows_in = address(x[b + db, :, cols(ch)].rearrange("(g p) t -> p g t", g=G))
                    need(sp, xl_rdy, done(1, b, c, 1, 0))
                    sp.dma_start(x_in[:, :, cols(ch)], rows_in).then_inc(x_ld[ch], 16)
                if finishing(b, c):
                    g = c - 2
                    rows_out = address(out[b - 1, g * P:(g + 1) * P, :])
                    need(sp, fin_rdy, final(b - 1, g, NCH - 1))
                    sp.dma_start(rows_out, x1[1 - par][:, g, :]).then_inc(out_st[g], 16)

            walk(sp, step)
            for g in range(G):
                sp.wait_ge(out_st[g], 16 * (B + 1))
            sp.wait_ge(w_ld, 16 * 10)
            sp.wait_ge(r_ld, 16 * 3)

        @block.gpsimd
        def _(pool):
            pool.memset(ident[:], 0.0).then_inc(consts, 1)
            pool.memset(ident_b[:], 0.0).then_inc(consts, 1)
            pool.memset(mask[:], 0.0).then_inc(consts, 1)
            pool.wait_ge(consts, 3)
            pool.affine_select(out=ident[:], in_=ident[:], compare_op=ALU.not_equal, fill=1.0, base=0,
                               pattern=[[-1, P]], channel_multiplier=1).then_inc(consts, 1)
            pool.affine_select(out=ident_b[:], in_=ident_b[:], compare_op=ALU.not_equal, fill=1.0, base=0,
                               pattern=[[-1, P]], channel_multiplier=1).then_inc(consts, 1)
            pool.wait_ge(consts, 5)
            for h in range(HPG):
                m = mask[SUB * h:SUB * (h + 1)]
                pool.affine_select(out=m, in_=m, compare_op=ALU.is_ge, fill=NEG, base=0,
                                   pattern=[[0, HALF], [1, KEYS]], channel_multiplier=-1).then_inc(consts, 1)
                pool.wait_ge(consts, 6 + 2 * h)
                pool.affine_select(out=m, in_=m, compare_op=ALU.is_ge, fill=NEG, base=WINDOW - 1,
                                   pattern=[[0, HALF], [-1, KEYS]], channel_multiplier=1).then_inc(consts, 1)
                pool.wait_ge(consts, 7 + 2 * h)
            pool.memset(ones, 1.0).then_inc(consts, 1)
            for rows in (keys, values):
                pool.memset(rows[:, :, 0:LEFT], 0.0).then_inc(zeros, 1)
                pool.memset(rows[:, :, LEFT + T:], 0.0).then_inc(zeros, 1)
            pool.memset(prob[:], 0.0).then_inc(zeros, 1)
            pool.wait_ge(zeros, 7)
            pool.memset(ex[E:E + 1, :], 1.0).then_inc(consts, 1)
            pool.wait_ge(consts, 15)

            NEWTON = 15

            def inverse_root(chain, base, mv, rs, neg_mean, ready):
                k = [0]

                def link(ins):
                    k[0] += 1
                    ins.then_inc(chain, 1)
                    pool.wait_ge(chain, base + k[0])
                    pool.tensor_tensor(pool_pad[:], ident[:, 0:1], ident[:, 0:1], ALU.mult)

                link(pool.tensor_scalar(half_var[:], mv[:, :, 1], EPS, None, ALU.add))
                link(pool.tensor_scalar(rs[:].bitcast(I32), half_var[:].bitcast(I32), -0.5, float(RSQRT_SEED),
                                       ALU.mult, ALU.add))
                link(pool.tensor_scalar(half_var[:], half_var[:], -0.5, None, ALU.mult))
                for _ in range(3):
                    link(pool.tensor_tensor(nt[:], rs[:], rs[:], ALU.mult))
                    link(pool.tensor_tensor(nt[:], nt[:], half_var[:], ALU.mult))
                    link(pool.tensor_scalar(nt[:], nt[:], 1.5, None, ALU.add))
                    link(pool.tensor_tensor(rs[:], rs[:], nt[:], ALU.mult))
                assert k[0] == NEWTON
                pool.tensor_scalar(neg_mean[:], mv[:, :, 0], -1.0, None, ALU.mult).then_inc(ready, 1)

            def ln1(b):
                need(pool, aggr1, (b + 1) * (G + 1))
                pool.tensor_tensor(pool_pad[:], ident[:, 0:1], ident[:, 0:1], ALU.mult)
                inverse_root(root1, b * NEWTON, mv_in, rs_in, neg_mean_in, ln1_rdy)

            def step(b, c, par):
                if isinstance(b, int) and b == -1 and c == 3:
                    ln1(0)
                if c == 3 and seq(b + 1) and live(b, c, 0):
                    ln1(b + 1)

                def x_low():
                    ch, _ = place(c, 1)
                    need(pool, xh_rdy, done(1, b, c, 1, 0))
                    pool.tensor_tensor(x_lo[:], x_in[:, :, cols(ch)], x_hi[:], ALU.subtract).then_inc(xl_rdy, 1)

                if live(b, c, 2):
                    need(pool, ch_rdy, done(1, b, c, 2, 0))
                    pool.tensor_tensor(c_lo[:], c_in[:], c_hi[:], ALU.subtract).then_inc(cl_rdy, 1)
                if live(b, c, 1) and c < 3:
                    x_low()

                if live(b, c, -1):
                    pch, db = place(c, -1)
                    rows = x1[(par if db == 0 else 1 - par)][:, 1, cols(pch)]
                    need(pool, ob_rdy, done(1, b, c, -1, 0))
                    need(pool, res_in, done(1, b, c, -1, 0) * 16)
                    pool.tensor_tensor(rows, rows, x_res[:, 1], ALU.add).then_inc(x1_rdy[1], 1)

                def normalise(u):
                    need(pool, iv_rdy, done(UNITS, b, c, 0, u))
                    pool.tensor_tensor(score[:, u], score[:, u],
                                       p_inv[:, u, :].unsqueeze(2).to_broadcast([P, HALF, KEYS]),
                                       ALU.mult).then_inc(pm_rdy, 1)

                def low(u):
                    need(pool, ph_rdy, done(UNITS, b, c, 0, u))
                    pool.tensor_tensor(part(prob[:, u % 2], 1)[:, :, 0:KEYS], score[:, u],
                                       part(prob[:, u % 2], 0)[:, :, 0:KEYS], ALU.subtract).then_inc(pl_rdy, 1)

                if live(b, c, 0):
                    normalise(0)
                    normalise(1)
                    low(0)
                    low(1)
                if live(b, c, 1) and c == 3:
                    x_low()
                if live(b, c, 0):
                    normalise(2)
                    normalise(3)
                    low(2)
                    low(3)

                if c == 0 and seq(b - 1):
                    need(pool, aggr2, b * (G + 1))
                    pool.tensor_tensor(pool_pad[:], ident[:, 0:1], ident[:, 0:1], ALU.mult)
                    inverse_root(root2, (b - 1) * NEWTON, mv_x1, rs_x1, neg_mean_x1, ln2_rdy)
            walk(pool, step)

        @block.scalar
        def _(act):
            act.wait_ge(w_ld, 16 * 10)
            act.activation(gate_a[:], gates[:, 0:1], ACT.Tanh).then_inc(gate_rdy, 1)
            act.activation(gate_f[:], gates[:, 1:2], ACT.Tanh).then_inc(gate_rdy, 1)
            act.wait_ge(gate_rdy, 3)
            for i, k in enumerate("kvo"):
                act.activation(w_hi[k][:], x1[1][:, :, i * C:(i + 1) * C], ACT.Copy,
                               ).then_inc(w_high, 1)
            act.wait_ge(zeros, 7)

            def step(b, c, par):
                def attention_high(g):
                    need(act, av_mm, done(2, b, c, -1, g))
                    need(act, o_mm, done(2, b, c, -2, 1))
                    need(act, al_rdy, done(2, b, c, -2, g))
                    act.activation(att_hi[:, g], ps_a[g][:], ACT.Copy,
                                   scale=v_unscale[:, (c - 1) % 2, g:g + 1]).then_inc(ah_rdy, 1)

                def spread_queries(g):
                    need(act, q_mm, done(2, b, c, 0, g))
                    need(act, s_mm, done(UNITS, b, c, -1, UNITS - 1))
                    for h in range(HPG):
                        r = slice(SUB * h, SUB * (h + 1))
                        act.activation(q_diag[r, g, :, r], ps_s[g][r, :].rearrange("p (n i) -> p n i", i=SUB),
                                       ACT.Identity, bias=bias["q"][r, g:g + 1]).then_inc(q_rdy, 1)

                if live(b, c, 0) and c in (0, 3):
                    spread_queries(0)
                if live(b, c, -1):
                    attention_high(0)
                if live(b, c, 0) and c in (1, 2):
                    spread_queries(0)
                if live(b, c, -1):
                    attention_high(1)
                if live(b, c, 0):
                    spread_queries(1)

                def centre():
                    ch, db = place(c, 1)
                    need(act, x_ld[ch], (b + db + 1) * 16)
                    need(act, ln1_rdy, b + db + 1)
                    for g in range(G):
                        act.activation(x_in[:, g, cols(ch)], x_in[:, g, cols(ch)], ACT.Identity,
                                       bias=neg_mean_in[:, g:g + 1]).then_inc(xc_rdy, 1)

                def x_high():
                    ch, _ = place(c, 1)
                    need(act, xc_rdy, done(2, b, c, 1, 1))
                    need(act, q_mm, done(2, b, c, 0, 1))
                    act.activation(x_hi[:], x_in[:, :, cols(ch)], ACT.Copy).then_inc(xh_rdy, 1)

                def exponent(u):
                    need(act, sh_rdy, done(UNITS, b, c, 0, u))
                    act.activation(score[:, u], score[:, u], ACT.Exp, scale=SCALE).then_inc(e_rdy, 1)

                def high(u):
                    need(act, pm_rdy, done(UNITS, b, c, 0, u))
                    need(act, pt_rdy, done(UNITS, b, c, 0, u - 2))
                    act.activation(part(prob[:, u % 2], 0)[:, :, 0:KEYS], score[:, u], ACT.Copy).then_inc(ph_rdy, 1)

                if live(b, c, 0):
                    for g in range(G):
                        if g == 0:
                            need(act, vs_rdy, done(3, b, c, 0, 2))
                        act.activation(part(v_pair[:, g], 0), values[:, g, c * CHUNK:(c + 1) * CHUNK + SUB],
                                       ACT.Copy, scale=v_scale[:, g:g + 1]).then_inc(vh_rdy, 1)
                if live(b, c, 0):
                    exponent(0)
                if live(b, c, 2):
                    need(act, ctx_in, done(1, b, c, 2, 0) * 16)
                    need(act, k_mm, done(2, b, c, 1, 1))
                    need(act, cl_rdy, done(1, b, c, 1, 0))
                    act.activation(c_hi[:], c_in[:], ACT.Copy).then_inc(ch_rdy, 1)
                if live(b, c, 1) and c < 3:
                    centre()
                if live(b, c, 0):
                    exponent(1)

                def output_bias():
                    ch, db = place(c, -1)
                    buf = x1[(par if db == 0 else 1 - par)]
                    need(act, o_mm, done(2, b, c, -1, 1))
                    if ch == 0:
                        need(act, out_st[1], b * 16)
                    act.activation(buf[:, 1, cols(ch)], ps_j[1][:], ACT.Identity,
                                   bias=bias["o"][:, 1:2]).then_inc(ob_rdy, 1)

                if live(b, c, 1) and c < 3:
                    x_high()
                if live(b, c, -1):
                    output_bias()
                if live(b, c, 1) and c == 3:
                    centre()
                    x_high()
                if c == 2 and seq(b - 1):
                    need(act, wt_mm, b)
                    act.activation(wd_t[:], ps_t[0:E + 1, 0:G * P].rearrange("e (g p) -> e g p", g=G),
                                   ACT.Copy).then_inc(wt_rdy, 1)
                def copy_rows(g):
                    need(act, t_mm, done(2, b, c, -1, g))
                    need(act, r_mm, done(1, b, c, -2, 0))
                    act.activation(x1_t[:, g], ps_t[:].rearrange("p (k t) -> p k t", k=TB), ACT.Copy).then_inc(xt_rdy, 1)

                ch, _ = place(c, 2)
                at = slice(LEFT + ch * CHUNK, LEFT + (ch + 1) * CHUNK)

                def copy_values(g):
                    need(act, v_mm, done(2, b, c, 2, g))
                    need(act, vl_rdy, done(2, b, c, -1, 1))
                    act.activation(values[:, g, at], ps_j[g][:], ACT.Identity,
                                   bias=bias["v"][:, g:g + 1]).then_inc(v_rdy, 1)

                def copy_keys(g):
                    need(act, k_mm, done(2, b, c, 2, g))
                    need(act, s_mm, done(UNITS, b, c, -1, UNITS - 1))
                    act.activation(keys[:, g, at], ps_j[g][:], ACT.Identity,
                                   bias=bias["k"][:, g:g + 1]).then_inc(k_rdy, 1)

                if live(b, c, 0):
                    exponent(2)
                    high(0)
                    exponent(3)
                if live(b, c, -1):
                    copy_rows(0)
                if live(b, c, 2):
                    copy_values(0)
                if live(b, c, 0):
                    high(1)
                if live(b, c, 2):
                    copy_values(1)
                if c == 1 and seq(b - 1):
                    need(act, lg_rdy, b * G)
                    for g in range(G):
                        for j in range(2):
                            act.activation(lg[:, g, j], lg[:, g, j], ACT.Exp, bias=neg_top[:, g:g + 1],
                                           accum_out=z_all[:, g, j:j + 1]).then_inc(le_rdy, 1)
                if c == 3 and seq(b + 1):
                    need(act, ln1_rdy, b + 2)
                    need(act, q_mm, done(2, b, c, 0, 1))
                    for g in range(G):
                        act.activation(w_hi["q"][:, g], wq_raw[:, g], ACT.Copy, scale=rs_in[:, g:g + 1]).then_inc(wqh_rdy, 1)
                if live(b, c, -1):
                    copy_rows(1)
                if live(b, c, 2):
                    copy_keys(0)
                if live(b, c, 0):
                    high(2)
                if live(b, c, 2):
                    copy_keys(1)
                if live(b, c, 0):
                    high(3)

            walk(act, step)

        @block.vector
        def _(dve):
            dve.memset(q_diag[:], 0.0).then_inc(zeros, 1)
            dve.memset(v_diag[:], 0.0).then_inc(zeros, 1)
            dve.wait_ge(gate_rdy, 2)
            dve.wait_ge(w_ld, 16 * 10)
            wo_staged = x1[1][:, :, 2 * C:3 * C]
            dve.tensor_scalar(wo_staged, wo_staged, gate_a[:], None, ALU.mult).then_inc(gate_rdy, 1)
            dve.tensor_scalar(bias["o"][:], bias["o"][:], gate_a[:], None, ALU.mult).then_inc(sum_rdy, 1)
            for i, k in enumerate("kvo"):
                dve.wait_ge(w_high, i + 1)
                dve.tensor_tensor(w_lo[k][:], x1[1][:, :, i * C:(i + 1) * C], w_hi[k][:], ALU.subtract).then_inc(w_low, 1)
            dve.memset(pad[:, 3:4], 0.0).then_inc(fin_rdy, NCH * G)
            for g in range(G):
                dve.memset(pad[:, 4 + g:5 + g], 0.0).then_inc(out_st[g], 16)

            dve.wait_ge(sum_rdy, 1)
            dve.wait_ge(zeros, 7)

            def stats_in(g, ch):
                dve.bn_stats(st_in[:, g, ch], x_in[:, g, cols(ch)]).then_inc(st1_rdy, 1)

            def aggregate_in(b):
                need(dve, st1_rdy, b * (NCH * G) + NCH * G)
                dve.memset(pad[:, 1:2], 0.0).then_inc(aggr1, 1)
                for g in range(G):
                    dve.bn_aggr(mv_in[:, g], st_in[:, g]).then_inc(aggr1, 1)

            for ch in range(NCH):
                dve.wait_ge(x_ld[ch], 16)
                for g in range(G):
                    stats_in(g, ch)
            aggregate_in(0)
            ROUTER = 12

            def step(b, c, par):
                def attention_low(g):
                    need(dve, ah_rdy, done(2, b, c, -1, g))
                    dve.scalar_tensor_tensor(att_lo[:, g], ps_a[g][:], v_unscale[:, (c - 1) % 2, g:g + 1],
                                             att_hi[:, g], ALU.mult, ALU.subtract).then_inc(al_rdy, 1)

                def values_low(g):
                    need(dve, vh_rdy, done(2, b, c, 0, g))
                    dve.scalar_tensor_tensor(part(v_pair[:, g], 1), values[:, g, c * CHUNK:(c + 1) * CHUNK + SUB],
                                             v_scale[:, g:g + 1], part(v_pair[:, g], 0),
                                             ALU.mult, ALU.subtract).then_inc(vl_rdy, 1)

                def spread(g, heads):
                    need(dve, vl_rdy, done(2, b, c, 0, g))
                    need(dve, av_mm, done(2, b, c, -1, g))
                    for h in heads:
                        r = slice(SUB * h, SUB * (h + 1))
                        dve.transpose(v_diag[r, g, :, r],
                                      v_pair[r, g].rearrange("p (n i) -> p n i", i=SUB)).then_inc(vd_rdy, 1)

                def scores_of(u):
                    return ps_s[u % 2][:, 0:HALF * KEYS].rearrange("p (n k) -> p n k", k=KEYS)

                def largest(u):
                    need(dve, s_mm, done(UNITS, b, c, 0, u))
                    dve.tensor_reduce(neg_max[:, u], scores_of(u), AX, ALU.max, negate=True).then_inc(mx_rdy, 1)

                def shift(u):
                    need(dve, mx_rdy, done(UNITS, b, c, 0, u))
                    need(dve, pl_rdy, done(UNITS, b, c, 0, u - SCORE_SLOTS))
                    dve.tensor_tensor(score[:, u], scores_of(u), neg_max[:, u, :].unsqueeze(2).to_broadcast([P, HALF, KEYS]),
                                      ALU.add).then_inc(sh_rdy, 1)

                def total(u):
                    need(dve, e_rdy, done(UNITS, b, c, 0, u))
                    dve.tensor_reduce(p_sum[:, u], score[:, u], AX, ALU.add).then_inc(su_rdy, 1)

                def invert(u):
                    need(dve, su_rdy, done(UNITS, b, c, 0, u))
                    dve.reciprocal(p_inv[:, u], p_sum[:, u]).then_inc(iv_rdy, 1)

                def turn(u):
                    need(dve, pl_rdy, done(UNITS, b, c, 0, u))
                    need(dve, av_mm, done(2, b, c, -1, u // 2))
                    dve.transpose(prob_t[:, u // 2, (u % 2) * CHUNK:(u % 2 + 1) * CHUNK],
                                  prob[:, u % 2].rearrange("p n k -> p (n k)")).then_inc(pt_rdy, 1)

                def residual():
                    g = 0
                    ch, db = place(c, -1)
                    buf = x1[(par if db == 0 else 1 - par)]
                    need(dve, o_mm, done(2, b, c, -1, g))
                    need(dve, res_in, done(1, b, c, -1, 0) * 16)
                    if ch == 0:
                        need(dve, out_st[g], b * 16)
                    dve.scalar_tensor_tensor(buf[:, g, cols(ch)], ps_j[g][:], bias["o"][:, g:g + 1], x_res[:, g],
                                             ALU.add, ALU.add).then_inc(x1_rdy[0], 1)

                def stats_x1(g):
                    ch, db = place(c, -1)
                    buf = x1[(par if db == 0 else 1 - par)]
                    need(dve, x1_rdy[g], done(1, b, c, -1, 0))
                    dve.bn_stats(st_x1[:, g, ch], buf[:, g, cols(ch)]).then_inc(st2_rdy, 1)

                def finish(j):
                    g, buf = c - 2, x1[1 - par]
                    need(dve, mix_mm, (b - 1) * (NCH * G) + NCH * g + j + 1)
                    dve.scalar_tensor_tensor(buf[:, g, cols(j)], buf[:, g, cols(j)], row_a[:, g:g + 1],
                                             ps_a[j % 2][:], ALU.mult, ALU.add).then_inc(fin_rdy, 1)

                def values_largest():
                    ch, _ = place(c, 2)
                    need(dve, v_rdy, done(2, b, c, 2, 1))
                    dve.tensor_reduce(v_max[:, :, ch], values[:, :, LEFT + ch * CHUNK:LEFT + (ch + 1) * CHUNK],
                                      AX, ALU.max, apply_absolute_value=True).then_inc(vm_rdy, 1)

                def values_scale(stage):
                    ch = c
                    first, last = max(ch - 1, 0), min(ch + 1, NCH - 1)
                    slot = v_unscale[:, ch % 2]
                    if stage == 0:
                        need(dve, vm_rdy, done(1, b, c, 1 if live(b, c, 1) else 0, 0))
                        dve.tensor_reduce(v_top[:], v_max[:, :, first:last + 1], AX, ALU.max).then_inc(vs_rdy, 1)
                    if stage == 1:
                        need(dve, vs_rdy, done(3, b, c, 0, 0))
                        dve.tensor_scalar(slot, v_top[:], TINY, 1.0 / TOP, ALU.max, ALU.mult).then_inc(vs_rdy, 1)
                    if stage == 2:
                        need(dve, vs_rdy, done(3, b, c, 0, 1))
                        dve.reciprocal(v_scale[:], slot).then_inc(vs_rdy, 1)

                if isinstance(b, int) and b == 0 and c == 0:
                    dve.wait_ge(sum_mm, 1)
                    dve.tensor_copy(wr_sum[:], ps_r[:, 0:E]).then_inc(sum_rdy, 1)
                if isinstance(b, int) and b == 0 and c == 1:
                    dve.wait_ge(sum_rdy, 2)
                now, before, stats = live(b, c, 0), live(b, c, -1), live(b, c, 4) and live(b, c, 0)
                if now:
                    values_scale(0)
                if stats:
                    ch, db = place(c, 4)
                    need(dve, x_ld[ch], (b + db + 1) * 16)
                    stats_in(0, ch)
                if now:
                    values_scale(1)
                if before:
                    attention_low(0)
                if now:
                    values_scale(2)
                if stats:
                    stats_in(1, ch)
                if before:
                    attention_low(1)
                if stats and c == 3:
                    aggregate_in(b + 1)
                if now:
                    largest(0)
                    shift(0)
                if before:
                    residual()
                if now:
                    values_low(0)
                    largest(1)
                    spread(0, (0,))
                    shift(1)
                    spread(0, (1, 2, 3))
                if before:
                    stats_x1(0)
                if now:
                    total(0)
                    largest(2)
                    invert(0)
                    shift(2)
                routing = c == 1 and seq(b - 1)
                if now:
                    total(1)
                if routing:
                    router_logits(b, 0)
                if now:
                    largest(3)
                if routing:
                    router_logits(b, 1)
                if now:
                    invert(1)
                    shift(3)
                if routing:
                    router_logits(b, 2)
                if now:
                    total(2)
                if before:
                    stats_x1(1)
                if c == 0 and seq(b - 1):
                    need(dve, st2_rdy, b * (NCH * G))
                    dve.memset(pad[:, 2:3], 0.0).then_inc(aggr2, 1)
                    for g in range(G):
                        dve.bn_aggr(mv_x1[:, g], st_x1[:, g]).then_inc(aggr2, 1)
                if routing:
                    router_logits(b, 3)
                if now:
                    values_low(1)
                    invert(2)
                    total(3)
                    turn(0)
                    invert(3)
                    spread(1, (0,))
                    turn(1)
                if finishing(b, c):
                    finish(0)
                    finish(1)
                if c == 3 and seq(b + 1):
                    need(dve, wqh_rdy, (b + 2) * G)
                    for g in range(G):
                        dve.scalar_tensor_tensor(w_lo["q"][:, g], wq_raw[:, g], rs_in[:, g:g + 1], w_hi["q"][:, g],
                                                 ALU.mult, ALU.subtract).then_inc(wql_rdy, 1)
                if live(b, c, 2):
                    values_largest()
                for k in range(HPG):
                    if now and k:
                        spread(1, (k,))
                    if routing:
                        router_weights(b, k)
                    if finishing(b, c) and k >= 2:
                        finish(k)
                for k in (0, 1):
                    if now:
                        turn(2 + k)
                    if routing:
                        router_weights(b, 4 + k)

            def router_logits(b, stage):
                base = (b - 1) * ROUTER
                if stage == 0:
                    need(dve, r_mm, (b - 1) * NCH + NCH)
                    need(dve, ln2_rdy, b)
                    for g in range(G):
                        dve.scalar_tensor_tensor(wd[:, g, 0:E], wr_sum[:], neg_mean_x1[:, g:g + 1],
                                                 ps_r[:, g * E:(g + 1) * E], ALU.mult, ALU.add).then_inc(small, 1)
                if stage == 1:
                    dve.wait_ge(small, base + 2)
                    for g in range(G):
                        dve.scalar_tensor_tensor(lg[:, g, 0], wd[:, g, 0:E], rs_x1[:, g:g + 1], rb[:],
                                                 ALU.mult, ALU.add).then_inc(small, 1)
                if stage == 2:
                    dve.wait_ge(small, base + 4)
                    dve.memset(pad[:, 0:1], 0.0).then_inc(small, 1)
                    for g in range(G):
                        dve.max(top[:, g], lg[:, g, 0]).then_inc(small, 1)
                if stage == 3:
                    dve.wait_ge(small, base + 7)
                    dve.tensor_scalar(neg_top[:], top[:, :, 0], -1.0, None, ALU.mult).then_inc(small, 1)
                    dve.match_replace(lg[:, 0, 1], top[:, 0], lg[:, 0, 0], NEG).then_inc(lg_rdy, 1)
                    dve.match_replace(lg[:, 1, 1], top[:, 1], lg[:, 1, 0], NEG).then_inc(lg_rdy, 1)

            def router_weights(b, stage):
                base = (b - 1) * ROUTER
                if stage == 0:
                    need(dve, le_rdy, b * (2 * G))
                    need(dve, lg_rdy, b * G)
                    dve.reciprocal(z_inv[:], z_all[:, :, 0]).then_inc(small, 1)
                    dve.tensor_tensor(wd[:, :, 0:E], lg[:, :, 0], lg[:, :, 1], ALU.subtract).then_inc(small, 1)
                if stage == 1:
                    dve.wait_ge(small, base + 10)
                    dve.tensor_scalar(z_inv[:], z_inv[:], gate_f[:], None, ALU.mult).then_inc(small, 1)
                if stage == 2:
                    dve.wait_ge(small, base + 11)
                    dve.tensor_tensor(wd[:, :, 0:E], wd[:, :, 0:E], z_inv[:].unsqueeze(2).to_broadcast([P, G, E]),
                                      ALU.mult).then_inc(small, 1)
                if stage == 3:
                    dve.wait_ge(small, base + 12)
                    dve.tensor_reduce(w_sum[:], wd[:, :, 0:E], AX, ALU.add).then_inc(wsum_rdy, 1)
                if stage == 4:
                    need(dve, wsum_rdy, 3 * b - 2)
                    dve.tensor_tensor(w_sum[:], w_sum[:], rs_x1[:], ALU.mult).then_inc(wsum_rdy, 1)
                if stage == 5:
                    need(dve, wsum_rdy, 3 * b - 1)
                    dve.tensor_scalar(row_a[:], w_sum[:], 1.0, None, ALU.add).then_inc(wsum_rdy, 1)
                    dve.tensor_tensor(wd[:, :, E:E + 1].rearrange("p g o -> p (g o)"), w_sum[:], neg_mean_x1[:],
                                      ALU.mult).then_inc(wd_rdy, 1)

            walk(dve, step)

        @block.tensor
        def _(pe):
            pe.wait_ge(consts, 15)
            pe.wait_ge(w_low, 3)

            def project(dst, k, g, hi, lo):
                o = slice(g * P, (g + 1) * P)
                terms = [(w_hi[k], hi), (w_lo[k], hi), (w_hi[k], lo)]
                n = 0
                for w, v in terms:
                    for i in range(G):
                        ins = pe.matmul(dst[:], w[:, i, o], v[:, i], start=(n == 0), stop=(n == 2 * G + 1))
                        n += 1
                return ins

            def step(b, c, par):
                def mixture(j):
                    g = c - 2
                    need(pe, wt_rdy, b)
                    if j < 2 and live(b, c, -1):
                        need(pe, al_rdy, done(2, b, c, -1, 1))
                    elif j < 2:
                        need(pe, al_rdy, 2 * N)
                        need(pe, fin_rdy, final(b - 1, g - 1, 2 + j) if g else 0)
                    else:
                        need(pe, fin_rdy, final(b - 1, g, j - 2))
                    pe.matmul(ps_a[j % 2][:], wd_t[:, g], ex[:, cols(j)], start=True, stop=True).then_inc(mix_mm, 1)

                def scores(u):
                    g, half = u // 2, u % 2
                    if u < 2:
                        need(pe, q_rdy, done(8, b, c, 0, 4 * u + 3))
                    else:
                        need(pe, sh_rdy, done(UNITS, b, c, 0, u - 2))
                    s = ps_s[u % 2]
                    pe.matmul(s[:, 0:HALF * KEYS], ident_b[:], mask[:].rearrange("p n k -> p (n k)"),
                              start=True, stop=False)
                    for n in range(HALF):
                        tb = half * HALF + n
                        at = c * CHUNK + tb * SUB
                        ins = pe.matmul(s[:, n * KEYS:(n + 1) * KEYS], q_diag[:, g, tb], keys[:, g, at:at + KEYS],
                                        start=False, stop=(n == HALF - 1))
                    ins.then_inc(s_mm, 1)

                def output(g):
                    if g == 0:
                        need(pe, al_rdy, done(2, b, c, -1, 1))
                    if live(b, c, 1):
                        need(pe, k_rdy, done(2, b, c, 1, g))
                    project(ps_j[g], "o", g, att_hi, att_lo).then_inc(o_mm, 1)

                def attend(g):
                    need(pe, pt_rdy, done(UNITS, b, c, -1, 2 * g + 1))
                    need(pe, vd_rdy, done(8, b, c, -1, 4 * g + 3))
                    need(pe, al_rdy, done(2, b, c, -2, g))
                    if c == 3 and seq(b - 1):
                        need(pe, fin_rdy, final(b - 1, 0, 2 + g))
                    if c == 0 and seq(b - 2):
                        need(pe, fin_rdy, final(b - 2, 1, 2 + g))
                    for j in range(NB + 1):
                        lo = max(0, (2 * j - 1) * SUB)
                        hi = min(2 * NB * SUB, (2 * j + 1) * SUB)
                        q0 = max(0, (j - 1) * SUB)
                        q1 = min(CHUNK, (j + 1) * SUB)
                        for n, (kv, kp) in enumerate(((0, 0), (1, 0), (0, 1))):
                            ins = pe.matmul(ps_a[g][:, q0:q1], part(v_diag[:, g, j], kv),
                                            part(prob_t[:, g, lo:hi], kp),
                                            start=(j == 0 and n == 0), stop=(j == NB), skip_group_check=True)
                    ins.then_inc(av_mm, 1)

                def queries():
                    for g in range(G):
                        need(pe, xl_rdy, done(1, b, c, 0, 0))
                        need(pe, wql_rdy, (b + 1) * G)
                        need(pe, sh_rdy, done(UNITS, b, c, -1, 2 + g))
                        project(ps_s[g], "q", g, x_hi, x_lo).then_inc(q_mm, 1)

                if live(b, c, 0) and c in (0, 3):
                    queries()
                if live(b, c, -1):
                    attend(0)
                if live(b, c, 0) and c in (1, 2):
                    queries()
                if live(b, c, -1):
                    attend(1)
                if live(b, c, 0):
                    need(pe, k_rdy, done(2, b, c, 1 if live(b, c, 1) else 0, 1))
                    scores(0)
                if live(b, c, -1):
                    output(0)
                if live(b, c, 0):
                    scores(1)
                if live(b, c, -1):
                    output(1)
                if c == 2 and seq(b - 1):
                    need(pe, wd_rdy, b)
                    need(pe, xt_rdy, done(2, b, c, -2, 1) if live(b, c, -2) else 2 * N)
                    for g in range(G):
                        ins = pe.transpose(ps_t[0:E + 1, g * P:(g + 1) * P], wd[:, g], ident[:])
                    ins.then_inc(wt_mm, 1)
                def rows(g):
                    ch, db = place(c, -1)
                    buf = x1[(par if db == 0 else 1 - par)]
                    need(pe, x1_rdy[g], done(1, b, c, -1, 0))
                    need(pe, xt_rdy, done(2, b, c, -1, g - 1))
                    if c == 2 and seq(b - 1):
                        need(pe, wt_rdy, b)
                    for k in range(TB):
                        t = ch * CHUNK + k * P
                        ins = pe.transpose(ps_t[:, k * P:(k + 1) * P], buf[:, g, t:t + P], ident[:])
                    ins.then_inc(t_mm, 1)

                if live(b, c, 0):
                    scores(2)
                if live(b, c, 0):
                    scores(3)
                if live(b, c, -2):
                    ch, db = place(c, -2)
                    need(pe, xt_rdy, done(2, b, c, -2, 1))
                    if ch == 0:
                        need(pe, lg_rdy, b * G)
                        if isinstance(b, int) and b == 0:
                            need(pe, sum_rdy, 2)
                    for k in range(TB):
                        for g in range(G):
                            ins = pe.matmul(ps_r[:, g * E:(g + 1) * E], x1_t[:, g, k], wr[:, ch * TB + k],
                                            start=(ch == 0 and k == 0 and g == 0),
                                            stop=(ch == NCH - 1 and k == TB - 1), skip_group_check=True)
                    ins.then_inc(r_mm, 1)
                if live(b, c, -1):
                    rows(0)
                if live(b, c, 2):
                    for g in range(G):
                        need(pe, cl_rdy, done(1, b, c, 2, 0))
                        if live(b, c, -1):
                            need(pe, ob_rdy if g else x1_rdy[0], done(1, b, c, -1, 0))
                        else:
                            need(pe, k_rdy, done(2, b, c, 1, g))
                        project(ps_j[g], "v", g, c_hi, c_lo).then_inc(v_mm, 1)
                if live(b, c, -1):
                    rows(1)
                if finishing(b, c):
                    mixture(0)
                    mixture(1)
                if live(b, c, 2):
                    for g in range(G):
                        need(pe, v_rdy, done(2, b, c, 2, g))
                        project(ps_j[g], "k", g, c_hi, c_lo).then_inc(k_mm, 1)
                if finishing(b, c):
                    mixture(2)
                    mixture(3)
                if isinstance(b, int) and b == -1 and c == 3:
                    pe.wait_ge(r_ld, 16 * 3)
                    for k in range(T // P):
                        ins = pe.matmul(ps_r[:, 0:E], ones, wr[:, k], start=(k == 0), stop=(k == T // P - 1))
                    ins.then_inc(sum_mm, 1)

            walk(pe, step)


def kernel(**inputs):
    import numpy as np
    import concourse.bacc as bacc
    from concourse import mybir as _mybir
    from concourse.bass_utils import run_bass_kernel_spmd as run

    a = {k: np.asarray(v) for k, v in inputs.items()}
    col = lambda v: np.ascontiguousarray(v.reshape(2, 128).T)
    arrays = {
        "x_dram": a["x"], "ctx_dram": a["ctx_4096"], "g_xattn_dram": a["g_xattn"], "g_ffn_dram": a["g_ffn"],
        "wqT_dram": a["L0_xattn_Wq"].T, "bq_dram": col(a["L0_xattn_bq"]),
        "wkT_dram": a["L0_xattn_Wk"].T, "bk_dram": col(a["L0_xattn_bk"]),
        "wvT_dram": a["L0_xattn_Wv"].T, "bv_dram": col(a["L0_xattn_bv"]),
        "woT_dram": a["L0_xattn_Wo"].T, "bo_dram": col(a["L0_xattn_bo"]),
        "wrT_dram": a["L0_ffn_router_weight"].T, "rbias_dram": a["L0_ffn_router_bias"],
        "experts_dram": a["L0_ffn_expert_bias"],
    }
    arrays = {k: np.ascontiguousarray(v) for k, v in arrays.items()}
    nc = bacc.Bacc("TRN2", target_bir_lowering=False, num_devices=1)
    args = [nc.dram_tensor(k, v.shape, _mybir.dt.from_np(v.dtype), kind="ExternalInput").ap() for k, v in arrays.items()]
    args.append(nc.dram_tensor("out_dram", a["x"].shape, _mybir.dt.float32, kind="ExternalOutput").ap())
    gated_window_attention_and_router(nc, *args)
    r = run(nc, [arrays], core_ids=[0])
    return r.results[0]["out_dram"]
```
